# Optimizing a Trainium2 kernel written in Bass

```python
import numpy as np
import jax
import jax.numpy as jnp

def _softmax(x, axis=-1):
    return jax.nn.softmax(x, axis=axis)

def _gelu(x):
    return jax.nn.gelu(x, approximate=True)

def _silu(x):
    return jax.nn.silu(x)

def _sigmoid(x):
    return jax.nn.sigmoid(x)

def _layernorm(x, axis=-1, eps=1e-05):
    m = jnp.mean(x, axis=axis, keepdims=True)
    v = jnp.var(x, axis=axis, keepdims=True)
    return (x - m) / jnp.sqrt(v + eps)

def _scatter_add(tgt, idx, src, axis=0):
    return tgt.at[idx].add(src)

def _segment_sum(src, seg, n):
    return jax.ops.segment_sum(src, seg, n)
kernel_name = 'mk_sandwich_d1_jaxref_r8_ed0aab'

def setup_inputs(seed: int=0):
    np.random.seed(seed)
    _w = jnp.asarray

    def _L0_attn_setup():
        import jax, jax.numpy as jnp
        import numpy as np
        NUM_HEAD = 16
        D_Q = 64
        D_KV = 64
        ROPE_BASE = 10000.0

        def _cos_sin(seq_len, dim):
            pos = jnp.arange(seq_len, dtype=jnp.float32)[:, None]
            ids = jnp.arange(dim // 2, dtype=jnp.float32)
            theta = ROPE_BASE ** (-2.0 * ids) / (dim // 2)
            r = pos * theta[None, :]
            return (jnp.cos(r), jnp.sin(r))

        def _rope(x, cos, sin):
            b, s, d = x.shape
            xv = x.reshape(b, s, d // 2, 2)
            x0, x1 = (xv[..., 0], xv[..., 1])
            out = jnp.stack([x0 * cos - x1 * sin, x1 * cos + x0 * sin], axis=-1)
            return out.reshape(b, s, d)
        key = jax.random.key(seed)
        ks = jax.random.split(key, 10)
        d_model, d_q, d_kv = (128, D_Q, D_KV)
        b, s = (2, 256)
        w = lambda k, i, o: jax.random.normal(k, (i, o), dtype=jnp.float32) * 0.02
        return {'x': jax.random.normal(ks[0], (b, s, d_model), dtype=jnp.float32), 'Wd_q_w': w(ks[1], d_model, d_q), 'Wd_q_b': jnp.zeros((d_q,), jnp.float32), 'Wu_q_w': w(ks[2], d_q, d_model), 'Wu_q_b': jnp.zeros((d_model,), jnp.float32), 'Wq_r_w': w(ks[3], d_q, d_model), 'Wq_r_b': jnp.zeros((d_model,), jnp.float32), 'Wk_r_w': w(ks[4], d_model, d_model), 'Wk_r_b': jnp.zeros((d_model,), jnp.float32), 'Wd_kv_w': w(ks[5], d_model, d_kv), 'Wd_kv_b': jnp.zeros((d_kv,), jnp.float32), 'Wu_k_w': w(ks[6], d_kv, d_model), 'Wu_k_b': jnp.zeros((d_model,), jnp.float32), 'Wu_v_w': w(ks[7], d_kv, d_model), 'Wu_v_b': jnp.zeros((d_model,), jnp.float32), 'Wo_w': w(ks[8], d_model, d_model), 'Wo_b': jnp.zeros((d_model,), jnp.float32)}
    _L0_attn_in = _L0_attn_setup()

    def _L0_ffn_setup():
        import jax, jax.numpy as jnp
        import numpy as np
        D_IN, D_HID = (128, 512)

        def _ternary(key, shape):
            return jax.random.randint(key, shape, -1, 2).astype(jnp.float32)

        def _tlin(x, w, s):
            return jnp.einsum('bsi,oi->bso', x, w) * s
        key = jax.random.key(seed)
        ks = jax.random.split(key, 12)
        inv = lambda fan: 1.0 / np.sqrt(fan).astype(np.float32)
        return {'x': jax.random.normal(ks[0], (4, 256, D_IN), dtype=jnp.float32), 'w1_w': _ternary(ks[1], (D_HID, D_IN)), 'w1_s': jax.random.uniform(ks[2], (D_HID,), dtype=jnp.float32) * inv(D_IN), 'w2_w': _ternary(ks[3], (D_HID, D_IN)), 'w2_s': jax.random.uniform(ks[4], (D_HID,), dtype=jnp.float32) * inv(D_IN), 'h1_w': _ternary(ks[5], (D_HID, D_HID)), 'h1_s': jax.random.uniform(ks[6], (D_HID,), dtype=jnp.float32) * inv(D_HID), 'h2_w': _ternary(ks[7], (D_HID, D_HID)), 'h2_s': jax.random.uniform(ks[8], (D_HID,), dtype=jnp.float32) * inv(D_HID), 'w3_w': _ternary(ks[9], (D_IN, D_HID)), 'w3_s': jax.random.uniform(ks[10], (D_IN,), dtype=jnp.float32) * inv(D_HID)}
    _L0_ffn_in = _L0_ffn_setup()
    _d = {'L0_attn_x': _L0_attn_in['x'], 'L0_attn_Wd_q_w': _L0_attn_in['Wd_q_w'], 'L0_attn_Wd_q_b': _L0_attn_in['Wd_q_b'], 'L0_attn_Wu_q_w': _L0_attn_in['Wu_q_w'], 'L0_attn_Wu_q_b': _L0_attn_in['Wu_q_b'], 'L0_attn_Wq_r_w': _L0_attn_in['Wq_r_w'], 'L0_attn_Wq_r_b': _L0_attn_in['Wq_r_b'], 'L0_attn_Wk_r_w': _L0_attn_in['Wk_r_w'], 'L0_attn_Wk_r_b': _L0_attn_in['Wk_r_b'], 'L0_attn_Wd_kv_w': _L0_attn_in['Wd_kv_w'], 'L0_attn_Wd_kv_b': _L0_attn_in['Wd_kv_b'], 'L0_attn_Wu_k_w': _L0_attn_in['Wu_k_w'], 'L0_attn_Wu_k_b': _L0_attn_in['Wu_k_b'], 'L0_attn_Wu_v_w': _L0_attn_in['Wu_v_w'], 'L0_attn_Wu_v_b': _L0_attn_in['Wu_v_b'], 'L0_attn_Wo_w': _L0_attn_in['Wo_w'], 'L0_attn_Wo_b': _L0_attn_in['Wo_b'], 'L0_ffn_w1_w': _L0_ffn_in['w1_w'], 'L0_ffn_w1_s': _L0_ffn_in['w1_s'], 'L0_ffn_w2_w': _L0_ffn_in['w2_w'], 'L0_ffn_w2_s': _L0_ffn_in['w2_s'], 'L0_ffn_h1_w': _L0_ffn_in['h1_w'], 'L0_ffn_h1_s': _L0_ffn_in['h1_s'], 'L0_ffn_h2_w': _L0_ffn_in['h2_w'], 'L0_ffn_h2_s': _L0_ffn_in['h2_s'], 'L0_ffn_w3_w': _L0_ffn_in['w3_w'], 'L0_ffn_w3_s': _L0_ffn_in['w3_s']}
    _x0 = _d['L0_attn_x']
    _d['L0_attn_x'] = jax.random.normal(jax.random.fold_in(jax.random.key(seed), 1), (1, 2048, 128), dtype=_x0.dtype)
    del _x0
    return _d

def reference(L0_attn_x, L0_attn_Wd_q_w, L0_attn_Wd_q_b, L0_attn_Wu_q_w, L0_attn_Wu_q_b, L0_attn_Wq_r_w, L0_attn_Wq_r_b, L0_attn_Wk_r_w, L0_attn_Wk_r_b, L0_attn_Wd_kv_w, L0_attn_Wd_kv_b, L0_attn_Wu_k_w, L0_attn_Wu_k_b, L0_attn_Wu_v_w, L0_attn_Wu_v_b, L0_attn_Wo_w, L0_attn_Wo_b, L0_ffn_w1_w, L0_ffn_w1_s, L0_ffn_w2_w, L0_ffn_w2_s, L0_ffn_h1_w, L0_ffn_h1_s, L0_ffn_h2_w, L0_ffn_h2_s, L0_ffn_w3_w, L0_ffn_w3_s):

    def _L0_attn_ref(x, Wd_q_w, Wd_q_b, Wu_q_w, Wu_q_b, Wq_r_w, Wq_r_b, Wk_r_w, Wk_r_b, Wd_kv_w, Wd_kv_b, Wu_k_w, Wu_k_b, Wu_v_w, Wu_v_b, Wo_w, Wo_b):
        import jax, jax.numpy as jnp
        import numpy as np
        NUM_HEAD = 16
        D_Q = 64
        D_KV = 64
        ROPE_BASE = 10000.0

        def _cos_sin(seq_len, dim):
            pos = jnp.arange(seq_len, dtype=jnp.float32)[:, None]
            ids = jnp.arange(dim // 2, dtype=jnp.float32)
            theta = ROPE_BASE ** (-2.0 * ids) / (dim // 2)
            r = pos * theta[None, :]
            return (jnp.cos(r), jnp.sin(r))

        def _rope(x, cos, sin):
            b, s, d = x.shape
            xv = x.reshape(b, s, d // 2, 2)
            x0, x1 = (xv[..., 0], xv[..., 1])
            out = jnp.stack([x0 * cos - x1 * sin, x1 * cos + x0 * sin], axis=-1)
            return out.reshape(b, s, d)
        b, s, d_model = x.shape
        h = NUM_HEAD
        hd = d_model // h
        scale = jnp.sqrt(jnp.float32(h + D_KV + D_Q))

        def heads(t):
            return t.reshape(b, s, h, hd).transpose(0, 2, 1, 3)
        cos, sin = _cos_sin(s, d_model)
        ct_q = x @ Wd_q_w + Wd_q_b
        qt_c = heads(ct_q @ Wu_q_w + Wu_q_b)
        qt_r = heads(_rope(ct_q @ Wq_r_w + Wq_r_b, cos, sin))
        query = qt_c + qt_r
        ct_kv = x @ Wd_kv_w + Wd_kv_b
        kt_c = heads(ct_kv @ Wu_k_w + Wu_k_b)
        kt_r = heads(_rope(x @ Wk_r_w + Wk_r_b, cos, sin))
        key = kt_c + kt_r
        value = heads(ct_kv @ Wu_v_w + Wu_v_b)
        attn = jnp.einsum('bhqd,bhkd->bhqk', query, key) / scale
        attn = jax.nn.softmax(attn, axis=-1)
        out = jnp.einsum('bhqk,bhkd->bhqd', attn, value)
        out = out.transpose(0, 2, 1, 3).reshape(b, s, d_model)
        return out @ Wo_w + Wo_b

    def _L0_ffn_ref(x, w1_w, w1_s, w2_w, w2_s, h1_w, h1_s, h2_w, h2_s, w3_w, w3_s):
        import jax, jax.numpy as jnp
        import numpy as np
        D_IN, D_HID = (128, 512)

        def _ternary(key, shape):
            return jax.random.randint(key, shape, -1, 2).astype(jnp.float32)

        def _tlin(x, w, s):
            return jnp.einsum('bsi,oi->bso', x, w) * s
        h = jax.nn.silu(_tlin(x, w1_w, w1_s)) * _tlin(x, w2_w, w2_s)
        h = jax.nn.gelu(_tlin(h, h1_w, h1_s), approximate=False)
        h = jax.nn.gelu(_tlin(h, h2_w, h2_s), approximate=False)
        return _tlin(h, w3_w, w3_s)
    x = L0_attn_x
    x = x + _layernorm(_L0_attn_ref(_layernorm(x, axis=-1), L0_attn_Wd_q_w, L0_attn_Wd_q_b, L0_attn_Wu_q_w, L0_attn_Wu_q_b, L0_attn_Wq_r_w, L0_attn_Wq_r_b, L0_attn_Wk_r_w, L0_attn_Wk_r_b, L0_attn_Wd_kv_w, L0_attn_Wd_kv_b, L0_attn_Wu_k_w, L0_attn_Wu_k_b, L0_attn_Wu_v_w, L0_attn_Wu_v_b, L0_attn_Wo_w, L0_attn_Wo_b), axis=-1)
    x = x + _layernorm(_L0_ffn_ref(_layernorm(x, axis=-1), L0_ffn_w1_w, L0_ffn_w1_s, L0_ffn_w2_w, L0_ffn_w2_s, L0_ffn_h1_w, L0_ffn_h1_s, L0_ffn_h2_w, L0_ffn_h2_s, L0_ffn_w3_w, L0_ffn_w3_s), axis=-1)
    return x

_drawn_inputs = setup_inputs


def setup_inputs(seed=0):
    import zlib

    import numpy as np

    out = dict(_drawn_inputs(seed))
    spreads = {'L0_attn_Wd_q_b': (0.0, 0.8),
     'L0_attn_Wu_q_b': (0.0, 0.8),
     'L0_attn_Wq_r_b': (0.0, 0.8),
     'L0_attn_Wk_r_b': (0.0, 0.8),
     'L0_attn_Wd_kv_b': (0.0, 0.347),
     'L0_attn_Wu_k_b': (0.0, 0.8),
     'L0_attn_Wu_v_b': (0.0, 0.1),
     'L0_attn_Wo_b': (0.0, 0.1)}
    factors = {'L0_attn_Wd_q_w': 8.0,
     'L0_attn_Wu_q_w': 8.0,
     'L0_attn_Wq_r_w': 8.0,
     'L0_attn_Wk_r_w': 8.0,
     'L0_attn_Wd_kv_w': 8.0,
     'L0_attn_Wu_k_w': 8.0}
    for name, (base, spread) in spreads.items():
        noise = np.random.default_rng([zlib.crc32(name.encode()), seed]).standard_normal(out[name].shape)
        drawn = base * np.exp(spread * noise) if base else spread * noise
        out[name] = jnp.asarray(drawn.astype(out[name].dtype))
    for name, factor in factors.items():
        out[name] = (out[name] * factor).astype(out[name].dtype)
    return out
```

```python
from contextlib import ExitStack

import concourse.bass as bass
from concourse import mybir
import numpy as np

T, D, H, HD, F = 2048, 128, 16, 8, 512
P = 128
BLK = 512
NB = T // BLK
NT = T // P
TPB = BLK // P
NG, GH = 4, 4
NI = NG * NB
VW = HD + 1
FC = F // P
SPLIT = 3
ROWS = SPLIT * SPLIT * HD
EPS = 1e-5
SCORE_SCALE = 1.0 / 12.0
SAFE_SCORE = 60.0
SAFE_PRODUCT = 0.98 * (SAFE_SCORE / SCORE_SCALE) ** 2

ONE_PAIR = float(np.array([0x3F803F80], np.uint32).view(np.float32)[0])

(W_D, W_QC, W_QR, W_QS, W_KC, W_KR, W_KS, W_V, B_V) = (D * n for n in range(9))
SEL = 9 * D
BIAS = SEL + H
SETUP_COLS = BIAS + 7
X_W1, X_W2 = 0, F
X_H1, X_H2 = 2 * F, 2 * F + FC * F
X_W3 = 2 * F + 2 * FC * F
X_WO = X_W3 + FC * D
X_BO = X_WO + NG * D
X_S = X_BO + D
TAIL_COLS = X_S + 4 * FC + 1


class Steps:

    def __init__(self, engine, sem):
        self.engine, self.sem, self.n = engine, sem, 0

    def mark(self, instruction):
        instruction.then_inc(self.sem, 1)
        self.n += 1
        return self.n

    def then_wait(self, instruction):
        self.engine.wait_ge(self.sem, self.mark(instruction))


def layer(nc, x_dram, setup_dram, tail_dram, cos_dram, sin_dram, ident_dram, q_scratch, k_scratch, out):
    fp32, bf16, int32 = mybir.dt.float32, mybir.dt.bfloat16, mybir.dt.int32
    ALU, ACT, AX = mybir.AluOpType, mybir.ActivationFunctionType, mybir.AxisListType
    ctx = ExitStack()
    with ctx:
        def sb(name, shape, dt=fp32):
            return ctx.enter_context(nc.sbuf_tensor(name, shape, dt))

        def sem(name):
            return ctx.enter_context(nc.semaphore(name))

        QT = sb("q_operand", [P, NI, GH, BLK], bf16)
        KT = sb("k_operand", [P, NG, GH, T], bf16)
        probs = sb("probs", [P, 4, GH, BLK])
        Qs = sb("q_split", [P, SPLIT, T], bf16)
        Ks = sb("k_split", [P, SPLIT, T], bf16)
        V = sb("v_all", [P, NT, NG, GH * VW])
        Vst = sb("v_group", [P, NT, GH * VW])
        attn = sb("attn", [P, NI, BLK // 32, HD])
        ident = sb("ident", [P, P])
        ident_bf = sb("ident_bf", [P, P], bf16)
        oT = sb("o_tokens", [P, BLK // 32, 32])
        rden = sb("rden", [P, BLK // 32, 1])
        stats = sb("stats", [P, NB, TPB, 6])
        mv = sb("mean_var", [P, NB, TPB, 2])
        rstd = sb("rstd", [P, NB, TPB])
        minus_half = sb("minus_half", [P, TPB])
        norm_max = sb("norm_max", [H, 2])
        norm_prod = sb("norm_prod", [H, 1])
        bound = sb("bound", [1, 1])
        unsafe = sb("unsafe", [1, 1], int32)
        half_max = sb("half_max", [P, GH * TPB, 2])
        neg_max = sb("neg_max", [P, GH * TPB])
        neg_rest = sb("neg_rest", [P, GH * TPB])
        shift_cols = sb("shift_cols", [P, P], bf16)
        shift_rows = sb("shift_rows", [SPLIT * GH * TPB, P], bf16)

        PS = ctx.enter_context(nc.psum_tensor("psum", [P, 8, BLK], fp32))
        ACC, M0, M1, M2 = 4, 5, 6, 7

        shift_parts = shift_cols[:, 0:SPLIT * GH * TPB].rearrange("p (s q) -> p s q", s=SPLIT)

        probs_f = probs[:, :, :, :].rearrange("p a b c -> p (a b c)")
        xs = probs_f[:, 0:T].rearrange("p (t d) -> p t d", d=D)
        xnT = probs_f[:, T:2 * T]
        ct = probs_f[:, 2 * T:3 * T]
        squares = probs_f[:, 3 * T:4 * T].bitcast(bf16).rearrange("p (s t) -> p s t", s=2)
        KT_f = KT[:, :, :, :].rearrange("p g j n -> p (g j n)").bitcast(fp32)
        QT_f = QT[:, :, :, :].rearrange("p i j n -> p (i j n)").bitcast(fp32)
        cosT, sinT = KT_f[:, 3 * 4096:3 * 4096 + T], KT_f[:, 3 * 4096 + T:4 * 4096]
        wp = KT_f[:, 2 * 4096:2 * 4096 + SETUP_COLS]
        tmp = QT_f[:, 3 * 4096:4 * 4096].rearrange("p (s k n) -> p s k n", s=2, n=BLK)
        sel_bf = QT_f[:, 2 * 4096:2 * 4096 + H // 2].bitcast(bf16)
        tw = QT_f[:, 0:TAIL_COLS]
        x1 = QT_f[:, 8192:8192 + T].rearrange("p (t d) -> p t d", d=D)
        xn2T = QT_f[:, 10240:10240 + T]
        ao = QT_f[:, 12288:12288 + BLK].rearrange("p (t d) -> p t d", d=D)
        ln = QT_f[:, 12800:12800 + BLK].rearrange("p (t d) -> p t d", d=D)
        ln2 = QT_f[:, 15360:15360 + BLK].rearrange("p (t d) -> p t d", d=D)
        silu = QT_f[:, 13312:13312 + 2 * BLK].rearrange("p (s n) -> p s n", n=BLK)
        yT = QT_f[:, 14336:14336 + 2 * BLK].rearrange("p (s n) -> p s n", n=BLK)
        hA = KT_f[:, 0:4 * T].rearrange("p (c t) -> p c t", c=FC)
        hB = KT_f[:, 4 * T:8 * T].rearrange("p (c t) -> p c t", c=FC)
        attn_pad = probs_f[:, 0:T].rearrange("p (g b d) -> p g b d", g=NG, d=32)
        oTn = probs_f[:, T:2 * T].rearrange("p (g n) -> p g n", g=NG)
        y_out = probs_f[:, 2 * T:3 * T].rearrange("p (t d) -> p t d", d=D)

        x_loaded = [sem(f"x_loaded{b}") for b in range(NB)]
        tables_loaded = [sem(f"tables_loaded{b}") for b in range(NB)]
        weights_loaded, ident_loaded, tail_loaded, x_again = (
            sem("weights_loaded"), sem("ident_loaded"), sem("tail_loaded"), sem("x_again"))
        stored = sem("stored")
        operands_in = sem("operands_in")
        dve = sem("dve_steps")
        pool = sem("pool_steps")
        pool_constants, dve_constants = sem("pool_constants"), sem("dve_constants")
        var_ready, rstd_ready, xn_ready = sem("var_ready"), sem("rstd_ready"), sem("xn_ready")
        xnT_psum, xnT_ready, ct_psum, ct_ready = sem("xnT_psum"), sem("xnT_ready"), sem("ct_psum"), sem("ct_ready")
        k_psum, v_psum, q_psum = sem("k_psum"), sem("v_psum"), sem("q_psum")
        k_drained, v_drained, q_drained = sem("k_drained"), sem("v_drained"), sem("q_drained")
        qk_ready, high_ready, squares_ready = sem("qk_ready"), sem("high_ready"), sem("squares_ready")
        rest_ready, mid_ready, low_ready = sem("rest_ready"), sem("mid_ready"), sem("low_ready")
        norms_psum, product_ready, product_psum, flag_ready = (
            sem("norms_psum"), sem("product_ready"), sem("product_psum"), sem("flag_ready"))
        k_pads, q_pads = sem("k_pads"), sem("q_pads")
        max_scores, max_reduced, max_steps = sem("max_scores"), sem("max_reduced"), sem("max_steps")
        shift_split, shift_psum, shift_rows_ready, shift_in = (
            sem("shift_split"), sem("shift_psum"), sem("shift_rows_ready"), sem("shift_in"))
        scores_ready, probs_ready, probs_used = sem("scores_ready"), sem("probs_ready"), sem("probs_used")
        v_staged, acc_free, attn_steps = sem("v_staged"), sem("acc_free"), sem("attn_steps")
        pad_zero, attn_padded, oTn_ready = sem("pad_zero"), sem("attn_padded"), sem("oTn_ready")
        proj_psum, proj_drained, ln2_ready = sem("proj_psum"), sem("proj_drained"), sem("ln2_ready")
        tail_var, tail_rstd = sem("tail_var"), sem("tail_rstd")
        xn2T_psum, xn2T_ready = sem("xn2T_psum"), sem("xn2T_ready")
        gate_psum, silu_ready, gated_ready = sem("gate_psum"), sem("silu_ready"), sem("gated_ready")
        hidden_psum, gelu_ready = sem("hidden_psum"), sem("gelu_ready")
        y_psum, yT_ready, y_tokens, y_drained, y_ready = (
            sem("y_psum"), sem("yT_ready"), sem("y_tokens"), sem("y_drained"), sem("y_ready"))
        out_done = sem("out_done")

        SIDES = (("k", Ks), ("q", Qs))
        G_DMAS = SPLIT * SPLIT + NB * SPLIT
        G0_DMAS = NB * SPLIT * (SPLIT + 1)

        def tokens(b):
            return slice(b * BLK, (b + 1) * BLK)

        def tiles(b):
            return slice(b * TPB, (b + 1) * TPB)

        def operands_of(g):
            return 16 * G0_DMAS + 16 * G_DMAS * g

        block = ctx.enter_context(nc.Block())

        @block.sync
        def _(sp):
            for b in range(NB):
                sp.dma_start(xs[:, tiles(b), :],
                             x_dram[tokens(b), :].rearrange("(t p) d -> p t d", p=P)).then_inc(x_loaded[b], 16)
            for b in range(NB):
                sp.dma_start(cosT[:, tokens(b)], cos_dram[:, tokens(b)]).then_inc(tables_loaded[b], 16)
                sp.dma_start(sinT[:, tokens(b)], sin_dram[:, tokens(b)]).then_inc(tables_loaded[b], 16)

            k_rows = k_scratch.rearrange("(g j d) a n -> g d a j n", g=NG, d=HD)
            q_rows = q_scratch.rearrange("(g j d) b n -> g (d b) j n", g=NG, d=HD)

            def lay_out_k(g, cols):
                for a in range(SPLIT):
                    for b in range(SPLIT):
                        r = SPLIT * HD * a + b
                        sp.dma_start(KT[r:r + SPLIT * HD - 2:SPLIT, g, :, cols],
                                     k_rows[g, :, a, :, cols]).then_inc(operands_in, 16)

            def lay_out_q(g, blk):
                for a in range(SPLIT):
                    r = SPLIT * HD * a
                    sp.dma_start(QT[r:r + SPLIT * HD, NB * g + blk, :, :],
                                 q_rows[g, :, :, tokens(blk)]).then_inc(operands_in, 16)

            sp.wait_ge(k_pads, 1)
            sp.wait_ge(q_pads, 1)
            for blk in range(NB):
                for s, (part, scratch) in enumerate(((Ks, k_scratch), (Qs, q_scratch))):
                    sp.wait_ge(low_ready, 2 * blk + s + 1)
                    sp.dma_start(scratch[:, :, tokens(blk)], part[:, :, tokens(blk)]).then_inc(stored, 16)
                sp.wait_ge(stored, 32 * (blk + 1))
                lay_out_k(0, tokens(blk))
                lay_out_q(0, blk)
            for g in range(1, NG):
                sp.wait_ge(k_pads, g + 1)
                sp.wait_ge(q_pads, g + 1)
                sp.wait_ge(operands_in, operands_of(g - 1))
                lay_out_k(g, slice(0, T))
                for blk in range(NB):
                    lay_out_q(g, blk)

            sp.wait_ge(flag_ready, 1)
            general = sp.value_load(unsafe[0:1, 0:1], min_val=0, max_val=1)
            with sp.If(general > 0):
                with sp.Fori(0, NI) as i:
                    sp.wait_ge(shift_rows_ready, i + 2)
                    for s in range(SPLIT):
                        n = GH * TPB
                        sp.dma_start(QT[ROWS + s:ROWS + s + 1, i, :, :].rearrange("p j n -> p (j n)"),
                                     shift_rows[n * s:n * s + n, :]).then_inc(shift_in, 16)

            sp.wait_ge(probs_used, NT * 8)
            sp.dma_start(tw, tail_dram[:, :]).then_inc(tail_loaded, 16)
            sp.wait_ge(probs_used, NT * 10)
            sp.dma_start(x1, x_dram[:, :].rearrange("(t p) d -> p t d", p=P)).then_inc(x_again, 16)
            for b in range(NB):
                sp.wait_ge(y_ready, b + 1)
                sp.dma_start(out[tokens(b), :].rearrange("(t p) d -> p t d", p=P),
                             y_out[:, tiles(b), :]).then_inc(out_done, 16)
            sp.wait_ge(out_done, 16 * NB)

        @block.gpsimd
        def _(gp):
            steps = Steps(gp, pool)
            k_pad = KT_f[64:P, :].rearrange("p (g n) -> p g n", g=NG)
            q_pad = QT_f[64:P, :].rearrange("p (g n) -> p g n", g=NG)
            nc.gpsimd.memset(minus_half[:, :], -0.5)
            nc.gpsimd.memset(V[:, :, :, :].rearrange("p t g (j w) -> p (t g j) w", w=VW)[:, :, HD:VW],
                             1.0).then_inc(pool_constants, 1)
            gp.wait_ge(pool_constants, 1)
            nc.gpsimd.memset(k_pad[:, 0, :], ONE_PAIR).then_inc(k_pads, 1)
            gp.wait_ge(k_pads, 1)

            def root(var, out_rstd, ready):
                steps.then_wait(nc.gpsimd.tensor_scalar(out_rstd, var, EPS, None, ALU.add))
                nc.gpsimd.tensor_tensor(out_rstd, out_rstd, minus_half[:, :], ALU.pow).then_inc(ready, 1)

            for b in range(NB):
                gp.wait_ge(var_ready, b + 1)
                root(mv[:, b, :, 1], rstd[:, b, :], rstd_ready)
            for n in range(2 * NB):
                b, s = divmod(n, 2)
                part = SIDES[s][1]
                gp.wait_ge(high_ready, n + 1)
                if n >= 2:
                    gp.wait_ge(mid_ready, n - 1)
                    gp.wait_ge(low_ready, n - 1)
                nc.gpsimd.tensor_tensor(tmp[:, s, 3, :], tmp[:, s, 2, :], part[:, 0, tokens(b)],
                                        ALU.subtract).then_inc(rest_ready, 1)
                gp.wait_ge(mid_ready, n + 1)
                nc.gpsimd.tensor_tensor(part[:, 2, tokens(b)], tmp[:, s, 3, :], part[:, 1, tokens(b)],
                                        ALU.subtract).then_inc(low_ready, 1)

            def stage_v(g, half):
                t = slice(half * NT // 2, (half + 1) * NT // 2)
                nc.gpsimd.tensor_copy(Vst[:, t, :], V[:, t, g, :]).then_inc(v_staged, 1)

            gp.wait_ge(v_drained, NB)
            stage_v(0, 0)
            stage_v(0, 1)
            gp.wait_ge(v_staged, 2)
            gp.wait_ge(low_ready, 2 * NB)
            gp.wait_ge(squares_ready, 2 * NB)
            gp.wait_ge(qk_ready, 2 * NB)
            gp.wait_ge(norms_psum, 2)
            for g in range(1, NG):
                nc.gpsimd.memset(k_pad[:, g, :], ONE_PAIR).then_inc(k_pads, 1)
                gp.wait_ge(k_pads, g + 1)
                nc.gpsimd.memset(q_pad[:, g, :], 0.0).then_inc(q_pads, 1)
                gp.wait_ge(q_pads, g + 1)
            with gp.Fori(1, NG) as g:
                gp.wait_ge(probs_used, NG * NT * g - NT // 2)
                stage_v(g, 0)
                gp.wait_ge(probs_used, NG * NT * g)
                stage_v(g, 1)

            gp.wait_ge(probs_used, NI * NT)
            steps.then_wait(nc.gpsimd.memset(attn_pad[:, :, :, :], 0.0))
            gp.wait_ge(attn_steps, 2 * NI)
            blocks = attn[:, :, :, :].rearrange("p (g b) t d -> p g b t d", g=NG)

            def tail_root(n):
                gp.wait_ge(tail_var, n + 1)
                root(mv[:, n % NB, :, 1], rstd[:, n % NB, :], tail_rstd)

            def pad(b):
                if b:
                    gp.wait_ge(oTn_ready, b)
                nc.gpsimd.tensor_copy(attn_pad[:, :, :, 0:HD], blocks[:, :, b, :, :]).then_inc(attn_padded, 1)

            pad(0)
            for b in range(NB):
                if b + 1 < NB:
                    pad(b + 1)
                tail_root(2 * b)
                tail_root(2 * b + 1)
            for b in range(NB):
                tail_root(2 * NB + b)

        @block.scalar
        def _(act):
            act.dma_start(wp, setup_dram[:, :]).then_inc(weights_loaded, 16)
            act.dma_start(ident[:, :], ident_dram[:, :]).then_inc(ident_loaded, 16)
            act.wait_ge(weights_loaded, 16)

            def drain_xnT(b):
                act.wait_ge(xnT_psum, b + 1)
                nc.scalar.activation(xnT[:, tokens(b)], PS[:, M0, :], ACT.Copy).then_inc(xnT_ready, 1)

            drain_xnT(0)
            for b in range(NB):
                act.wait_ge(ct_psum, b + 1)
                nc.scalar.activation(ct[:, tokens(b)], PS[:, M1, :], ACT.Identity,
                                     bias=wp[:, BIAS:BIAS + 1]).then_inc(ct_ready, 1)
                if b + 1 < NB:
                    drain_xnT(b + 1)
                for s, (_, part) in enumerate(SIDES):
                    n = 2 * b + s
                    act.wait_ge(qk_ready, n + 1)
                    nc.scalar.activation(part[:, 0, tokens(b)], tmp[:, s, 2, :], ACT.Copy).then_inc(high_ready, 1)
                    nc.scalar.activation(squares[:, s, tokens(b)], tmp[:, s, 2, :],
                                         ACT.Square).then_inc(squares_ready, 1)
                    act.wait_ge(rest_ready, n + 1)
                    nc.scalar.activation(part[:, 1, tokens(b)], tmp[:, s, 3, :], ACT.Copy).then_inc(mid_ready, 1)

            act.wait_ge(norms_psum, 2)

            def exps(t, slot, used=None):
                if used is not None:
                    act.wait_ge(probs_used, used)
                for half in range(2):
                    act.wait_ge(scores_ready, 2 * t + half + 1)
                    u = slice(2 * half, 2 * half + 2)
                    nc.scalar.activation(probs[:, slot, u, :], PS[:, u, :], ACT.Exp,
                                         scale=SCORE_SCALE).then_inc(probs_ready, 1)

            for t in range(4):
                exps(t, t)
            with act.Fori(1, NI * NT // 4) as r:
                for c in range(4):
                    exps(4 * r + c, c, 4 * r + c - 3)

            def drain_xn2T(b):
                act.wait_ge(xn2T_psum, b + 1)
                nc.scalar.activation(xn2T[:, tokens(b)], PS[:, M1, :], ACT.Copy).then_inc(xn2T_ready, 1)

            act.wait_ge(tail_loaded, 16)
            drain_xn2T(0)
            for b in range(NB):
                for c in range(FC):
                    n, slot = FC * b + c, c % 2
                    act.wait_ge(gate_psum, 2 * n + 1)
                    if n >= 2:
                        act.wait_ge(gated_ready, n - 1)
                    nc.scalar.activation(silu[:, slot, :], PS[:, slot, :], ACT.Silu,
                                         scale=tw[:, X_S + c:X_S + c + 1]).then_inc(silu_ready, 1)
                if b + 1 < NB:
                    drain_xn2T(b + 1)
            for layer_n, (dst, col) in enumerate(((hB, X_S + 2 * FC), (hA, X_S + 3 * FC))):
                with act.Fori(0, NB) as b:
                    for c in range(FC):
                        act.wait_ge(hidden_psum, FC * b + (FC * NB * layer_n + c + 1))
                        nc.scalar.activation(dst[:, c, bass.ds(b * BLK, BLK)], PS[:, 4 + c, :], ACT.Gelu,
                                             scale=tw[:, col + c:col + c + 1]).then_inc(gelu_ready, 1)
            for b in range(NB):
                act.wait_ge(y_psum, b + 1)
                if b >= 2:
                    act.wait_ge(y_tokens, b - 1)
                nc.scalar.activation(yT[:, b % 2, :], PS[:, b % 2, :], ACT.Copy,
                                     scale=tw[:, X_S + 4 * FC:X_S + 4 * FC + 1]).then_inc(yT_ready, 1)

        @block.vector
        def _(ve):
            steps = Steps(ve, dve)
            q_pad = QT_f[64:P, :].rearrange("p (g n) -> p g n", g=NG)
            nc.vector.memset(q_pad[:, 0, :], 0.0).then_inc(q_pads, 1)
            for b in range(NB):
                ve.wait_ge(x_loaded[b], 16)
                for t in range(TPB):
                    last = nc.vector.bn_stats(stats[:, b, t, :], xs[:, TPB * b + t, :])
                steps.then_wait(last)
                for t in range(TPB):
                    last = nc.vector.bn_aggr(mv[:, b, t, :], stats[:, b, t, :])
                last.then_inc(var_ready, 1)

            def normalise(b):
                ve.wait_ge(rstd_ready, b + 1)
                for t in range(TPB):
                    last = nc.vector.tensor_scalar(xs[:, TPB * b + t, :], xs[:, TPB * b + t, :], mv[:, b, t, 0:1],
                                                   rstd[:, b, t:t + 1], ALU.subtract, ALU.mult)
                last.then_inc(xn_ready, 1)

            def side(b, s, banks, psum, drained, bias):
                n = 2 * b + s
                content, rotated, swapped = banks
                t1, t2, whole = (tmp[:, s, k, :] for k in range(3))
                ve.wait_ge(psum, b + 1)
                steps.mark(nc.vector.scalar_tensor_tensor(t1, PS[:, rotated, :], wp[:, bias + 1:bias + 2],
                                                          cosT[:, tokens(b)], ALU.add, ALU.mult))
                nc.vector.scalar_tensor_tensor(t2, PS[:, swapped, :], wp[:, bias + 2:bias + 3],
                                               sinT[:, tokens(b)], ALU.add, ALU.mult)
                ve.wait_ge(dve, steps.n)
                nc.vector.scalar_tensor_tensor(t1, PS[:, content, :], wp[:, bias:bias + 1], t1,
                                               ALU.add, ALU.add).then_inc(drained, 1)
                ve.wait_ge(drained, b + 1)
                if n >= 2:
                    ve.wait_ge(squares_ready, n - 1)
                    ve.wait_ge(rest_ready, n - 1)
                nc.vector.tensor_tensor(whole, t1, t2, ALU.add).then_inc(qk_ready, 1)

            def values(b):
                ve.wait_ge(v_psum, b + 1)
                if b == 0:
                    ve.wait_ge(pool_constants, 1)
                for t in range(TPB):
                    last = nc.vector.tensor_tensor(
                        V[:, TPB * b + t, :, :].rearrange("p g (j w) -> p (g j) w", w=VW)[:, :, 0:HD],
                        PS[:, M1, D * t:D * (t + 1)].rearrange("p (h d) -> p h d", d=HD),
                        wp[:, B_V:B_V + D].rearrange("p (h d) -> p h d", d=HD), ALU.add)
                last.then_inc(v_drained, 1)

            normalise(0)
            ve.wait_ge(ident_loaded, 16)
            nc.vector.tensor_copy(ident_bf[:, :], ident[:, :]).then_inc(dve_constants, 1)
            normalise(1)
            ve.wait_ge(weights_loaded, 16)
            nc.vector.tensor_copy(sel_bf, wp[:, SEL:SEL + H]).then_inc(dve_constants, 1)
            for b in range(NB):
                ve.wait_ge(tables_loaded[b], 32)
                side(b, 0, (3, ACC, M2), k_psum, k_drained, BIAS + 4)
                values(b)
                if b + 2 < NB:
                    normalise(b + 2)
                side(b, 1, (0, 1, 2), q_psum, q_drained, BIAS + 1)

            for s in range(2):
                ve.wait_ge(norms_psum, s + 1)
                steps.mark(nc.vector.reduce_max(norm_max[:, s:s + 1], PS[0:H, 4 * s:4 * s + 4, :], AX.XY))
            ve.wait_ge(dve, steps.n)
            nc.vector.tensor_tensor(norm_prod[:, :], norm_max[:, 0:1], norm_max[:, 1:2],
                                    ALU.mult).then_inc(product_ready, 1)
            nc.vector.memset(PS[:, ACC, :], 0.0).then_inc(acc_free, 1)
            ve.wait_ge(product_psum, 1)
            steps.then_wait(nc.vector.reduce_max(bound[:, :], PS[0:1, 0, 0:H], AX.X))
            nc.vector.tensor_scalar(unsafe[:, :], bound[:, :], SAFE_PRODUCT, None, ALU.is_gt).then_inc(flag_ready, 1)
            ve.wait_ge(flag_ready, 1)
            general = ve.value_load(unsafe[0:1, 0:1], min_val=0, max_val=1)
            with ve.If(general > 0):
                nq = GH * TPB
                nc.vector.memset(shift_cols[:, :], 0.0).then_inc(shift_rows_ready, 1)
                ve.wait_ge(shift_rows_ready, 1)
                with ve.Fori(0, NI) as i:
                    for u in range(2 * nq):
                        ve.wait_ge(max_scores, 2 * nq * i + (u + 1))
                        h = u % 2
                        nc.vector.tensor_reduce(half_max[:, u // 2, h:h + 1], PS[:, 2 * h:2 * h + 2, :], AX.XY,
                                                ALU.max, negate=True).then_inc(max_reduced, 1)
                    ve.wait_ge(max_reduced, 2 * nq * i + 2 * nq)
                    nc.vector.tensor_tensor(neg_max[:, :], half_max[:, :, 0], half_max[:, :, 1],
                                            ALU.min).then_inc(max_steps, 1)
                    ve.wait_ge(max_steps, 5 * i + 1)
                    nc.vector.tensor_copy(shift_parts[:, 0, :], neg_max[:, :]).then_inc(max_steps, 1)
                    ve.wait_ge(max_steps, 5 * i + 2)
                    nc.vector.tensor_tensor(neg_rest[:, :], neg_max[:, :], shift_parts[:, 0, :],
                                            ALU.subtract).then_inc(max_steps, 1)
                    ve.wait_ge(max_steps, 5 * i + 3)
                    nc.vector.tensor_copy(shift_parts[:, 1, :], neg_rest[:, :]).then_inc(max_steps, 1)
                    ve.wait_ge(max_steps, 5 * i + 4)
                    nc.vector.tensor_tensor(shift_parts[:, 2, :], neg_rest[:, :], shift_parts[:, 1, :],
                                            ALU.subtract).then_inc(max_steps, 1)
                    ve.wait_ge(shift_psum, i + 1)
                    nc.vector.tensor_copy(shift_rows[:, :], PS[0:SPLIT * nq, M0, 0:P // 2].bitcast(bf16)
                                          ).then_inc(shift_rows_ready, 1)
                    ve.wait_ge(shift_in, 16 * SPLIT * i + 16 * SPLIT)

            with ve.Fori(0, NI) as i:
                ve.wait_ge(probs_used, NT * i + NT)
                nc.vector.transpose(oT[:, :, :].rearrange("p b d -> p (b d)"), PS[:, ACC, :]).then_inc(acc_free, 1)
                ve.wait_ge(acc_free, i + 2)
                nc.vector.reciprocal(rden[:, :, :], oT[:, :, HD:VW]).then_inc(attn_steps, 1)
                ve.wait_ge(attn_steps, 2 * i + 1)
                nc.vector.tensor_tensor(attn[:, i, :, :], oT[:, :, 0:HD],
                                        rden[:, :, :].to_broadcast([P, BLK // 32, HD]),
                                        ALU.mult).then_inc(attn_steps, 1)
                ve.wait_ge(attn_steps, 2 * i + 2)

            def statistics(n, src):
                for t in range(TPB):
                    last = nc.vector.bn_stats(stats[:, 0, t, :], src[:, t, :])
                steps.then_wait(last)
                for t in range(TPB):
                    last = nc.vector.bn_aggr(mv[:, n % NB, t, :], stats[:, 0, t, :])
                last.then_inc(tail_var, 1)

            def apply_norm(n, dst, src):
                ve.wait_ge(tail_rstd, n + 1)
                for t in range(TPB):
                    last = nc.vector.tensor_scalar(dst[:, t, :], src[:, t, :], mv[:, n % NB, t, 0:1],
                                                   rstd[:, n % NB, t:t + 1], ALU.subtract, ALU.mult)
                return last

            def untranspose(b):
                ve.wait_ge(attn_padded, b + 1)
                if b:
                    ve.wait_ge(proj_psum, b)
                nc.vector.transpose(oTn[:, :, :].rearrange("p g n -> p (g n)"),
                                    attn_pad[:, :, :, :].rearrange("p g b d -> p (g b d)")).then_inc(oTn_ready, 1)

            def attn_out(b):
                ve.wait_ge(proj_psum, b + 1)
                ve.wait_ge(tail_loaded, 16)
                for t in range(TPB):
                    last = nc.vector.tensor_tensor(ao[:, t, :], PS[:, M0, D * t:D * (t + 1)], tw[:, X_BO:X_BO + D],
                                                   ALU.add)
                last.then_inc(proj_drained, 1)
                ve.wait_ge(proj_drained, b + 1)
                statistics(2 * b, ao)

            def residual(b):
                steps.then_wait(apply_norm(2 * b, ln, ao))
                ve.wait_ge(x_again, 16)
                steps.then_wait(nc.vector.tensor_tensor(x1[:, tiles(b), :], x1[:, tiles(b), :], ln[:, :, :], ALU.add))
                statistics(2 * b + 1, x1[:, tiles(b), :])

            def second_norm(b):
                if b:
                    ve.wait_ge(xn2T_psum, b)
                apply_norm(2 * b + 1, ln2, x1[:, tiles(b), :]).then_inc(ln2_ready, 1)

            def gate(b, c):
                n, slot = FC * b + c, c % 2
                ve.wait_ge(gate_psum, 2 * n + 2)
                ve.wait_ge(silu_ready, n + 1)
                nc.vector.scalar_tensor_tensor(hA[:, c, tokens(b)], PS[:, 2 + slot, :],
                                               tw[:, X_S + FC + c:X_S + FC + c + 1], silu[:, slot, :],
                                               ALU.mult, ALU.mult).then_inc(gated_ready, 1)

            for stage in (untranspose, attn_out, residual, second_norm):
                stage(0)
            for b in range(NB):
                after = {0: attn_out, 1: residual} if b + 1 < NB else {}
                if after:
                    untranspose(b + 1)
                for c in range(FC):
                    gate(b, c)
                    if c in after:
                        after[c](b + 1)
                if after:
                    second_norm(b + 1)
            for b in range(NB):
                n = 2 * NB + b
                ve.wait_ge(y_tokens, b + 1)
                y = PS[:, 2 + b % 2, :].rearrange("p (t d) -> p t d", d=D)
                statistics(n, y)
                apply_norm(n, ln, y).then_inc(y_drained, 1)
                ve.wait_ge(y_drained, b + 1)
                nc.vector.tensor_tensor(y_out[:, tiles(b), :], x1[:, tiles(b), :], ln[:, :, :],
                                        ALU.add).then_inc(y_ready, 1)
                ve.wait_ge(y_ready, b + 1)

        @block.tensor
        def _(pe):
            mm = nc.tensor.matmul

            def weight(col):
                return wp[:, col:col + D]

            def transpose_tiles(bank, src):
                for t in range(TPB):
                    last = nc.tensor.transpose(PS[:, bank, D * t:D * (t + 1)], src[:, t, :], ident[:, :])
                return last

            def transpose_x(b):
                pe.wait_ge(xn_ready, b + 1)
                if b:
                    pe.wait_ge(xnT_ready, b)
                transpose_tiles(M0, xs[:, tiles(b), :]).then_inc(xnT_psum, 1)

            pe.wait_ge(ident_loaded, 16)
            transpose_x(0)
            pe.wait_ge(weights_loaded, 16)
            for b in range(NB):
                pe.wait_ge(xnT_ready, b + 1)
                if b:
                    pe.wait_ge(v_drained, b)
                mm(PS[:, M1, :], weight(W_D), xnT[:, tokens(b)], start=True, stop=True).then_inc(ct_psum, 1)
                if b + 1 < NB:
                    transpose_x(b + 1)
                if b:
                    pe.wait_ge(k_drained, b)
                mm(PS[:, ACC, :], weight(W_KR), xnT[:, tokens(b)], start=True, stop=True)
                mm(PS[:, M2, :], weight(W_KS), xnT[:, tokens(b)], start=True, stop=True)
                pe.wait_ge(ct_ready, b + 1)
                mm(PS[:, 3, :], weight(W_KC), ct[:, tokens(b)], start=True, stop=True).then_inc(k_psum, 1)
                for t in range(TPB):
                    at = b * BLK + t * P
                    last = mm(PS[:, M1, D * t:D * (t + 1)], ct[:, at:at + P], weight(W_V), start=True, stop=True)
                last.then_inc(v_psum, 1)
                if b:
                    pe.wait_ge(q_drained, b)
                mm(PS[:, 1, :], weight(W_QR), ct[:, tokens(b)], start=True, stop=True)
                mm(PS[:, 2, :], weight(W_QS), ct[:, tokens(b)], start=True, stop=True)
                mm(PS[:, 0, :], weight(W_QC), ct[:, tokens(b)], start=True, stop=True).then_inc(q_psum, 1)

            pe.wait_ge(dve_constants, 2)
            pe.wait_ge(k_drained, NB)
            pe.wait_ge(q_drained, NB)
            pe.wait_ge(v_drained, NB)
            pe.wait_ge(squares_ready, 2 * NB)
            for s in range(2):
                for b in range(NB):
                    last = mm(PS[0:H, 4 * s + b, :], sel_bf, squares[:, s, tokens(b)], start=True, stop=True)
                last.then_inc(norms_psum, 1)
            pe.wait_ge(product_ready, 1)
            mm(PS[0:1, 0, 0:H], norm_prod[:, :], ident[0:H, 0:H], start=True, stop=True).then_inc(product_psum, 1)

            pe.wait_ge(flag_ready, 1)
            general = pe.value_load(unsafe[0:1, 0:1], min_val=0, max_val=1)
            with pe.If(general > 0):
                nq = GH * TPB
                pe.wait_ge(operands_in, operands_of(NG - 1))
                with pe.Fori(0, NI) as i:
                    for u in range(2 * nq):
                        j, t, h = u // (2 * TPB), u // 2 % TPB, u % 2
                        if u >= 2:
                            pe.wait_ge(max_reduced, 2 * nq * i + (u - 1))
                        for k in range(2):
                            last = mm(PS[:, 2 * h + k, :], QT[:, i, j, P * t:P * (t + 1)],
                                      KT[:, i // NB, j, (2 * h + k) * BLK:(2 * h + k + 1) * BLK],
                                      start=True, stop=True)
                        last.then_inc(max_scores, 1)
                    pe.wait_ge(max_steps, 5 * i + 5)
                    pe.wait_ge(shift_rows_ready, i + 1)
                    nc.tensor.transpose(PS[:, M0, 0:P // 2].bitcast(bf16), shift_cols[:, :],
                                        ident_bf[:, :]).then_inc(shift_psum, 1)
                pe.wait_ge(shift_in, 16 * SPLIT * NI)

            def fill(i, t, half, n):
                for j in (2 * half, 2 * half + 1):
                    last = mm(PS[:, j, :], KT[:, i // NB, j, P * t:P * (t + 1)], QT[:, i, j, :],
                              start=True, stop=True)
                last.then_inc(scores_ready, 1)

            def attend(i, first, last_iteration):
                for t in range(NT):
                    ahead = t + 2
                    fi, ft = (i, ahead) if ahead < NT else (i + 1, ahead - NT)
                    filling = ahead < NT or not last_iteration
                    if filling:
                        if ahead == NT:
                            pe.wait_ge(operands_in, operands_of(fi // NB))
                        pe.wait_ge(probs_ready, 2 * NT * i + (2 * ahead - 1))
                        fill(fi, ft, 0, None)
                    pe.wait_ge(probs_ready, 2 * NT * i + (2 * t + 2))
                    if t == 0:
                        pe.wait_ge(acc_free, i + 1)
                        pe.wait_ge(v_staged, 2 * (i // NB) + 1)
                    if t == NT // 2:
                        pe.wait_ge(v_staged, 2 * (i // NB) + 2)
                    for j in range(GH):
                        last = mm(PS[32 * j:32 * j + VW, ACC, :], Vst[:, t, VW * j:VW * (j + 1)], probs[:, t % 4, j, :],
                                  start=t == 0, stop=t == NT - 1)
                    last.then_inc(probs_used, 1)
                    if filling:
                        pe.wait_ge(probs_ready, 2 * NT * i + 2 * ahead)
                        fill(fi, ft, 1, None)

            pe.wait_ge(operands_in, operands_of(0))
            fill(0, 0, 0, 0)
            fill(0, 0, 1, 1)
            pe.wait_ge(probs_ready, 1)
            fill(0, 1, 0, 2)
            pe.wait_ge(probs_ready, 2)
            fill(0, 1, 1, 3)
            with pe.Fori(0, NI - 1) as i:
                attend(i, False, False)
            attend(NI - 1, False, True)

            def project(b):
                pe.wait_ge(oTn_ready, b + 1)
                pe.wait_ge(tail_loaded, 16)
                if b:
                    pe.wait_ge(proj_drained, b)
                for t in range(TPB):
                    for g in range(NG):
                        last = mm(PS[:, M0, D * t:D * (t + 1)], oTn[:, g, P * t:P * (t + 1)],
                                  tw[:, X_WO + D * g:X_WO + D * (g + 1)], start=g == 0, stop=g == NG - 1)
                last.then_inc(proj_psum, 1)

            def transpose_x2(b):
                pe.wait_ge(ln2_ready, b + 1)
                if b:
                    pe.wait_ge(xn2T_ready, b)
                transpose_tiles(M1, ln2).then_inc(xn2T_psum, 1)

            def gates(b, c):
                n, slot = FC * b + c, c % 2
                pe.wait_ge(xn2T_ready, b + 1)
                if n >= 2:
                    pe.wait_ge(silu_ready, n - 1)
                mm(PS[:, slot, :], tw[:, X_W1 + P * c:X_W1 + P * (c + 1)], xn2T[:, tokens(b)],
                   start=True, stop=True).then_inc(gate_psum, 1)
                if n >= 2:
                    pe.wait_ge(gated_ready, n - 1)
                mm(PS[:, 2 + slot, :], tw[:, X_W2 + P * c:X_W2 + P * (c + 1)], xn2T[:, tokens(b)],
                   start=True, stop=True).then_inc(gate_psum, 1)

            project(0)
            transpose_x2(0)
            for b in range(NB):
                for c in range(FC):
                    gates(b, c)
                    if c == 0 and b + 1 < NB:
                        project(b + 1)
                if b + 1 < NB:
                    transpose_x2(b + 1)

            def hidden(b, src, w, drained):
                for c in range(FC):
                    if drained is not None:
                        pe.wait_ge(gelu_ready, drained + c)
                    for k in range(FC):
                        at = w + F * k + P * c
                        rhs = src[:, k, tokens(b)] if isinstance(b, int) else src[:, k, bass.ds(b * BLK, BLK)]
                        last = mm(PS[:, 4 + c, :], tw[:, at:at + P], rhs, start=k == 0, stop=k == FC - 1)
                    last.then_inc(hidden_psum, 1)

            pe.wait_ge(gated_ready, FC)
            hidden(0, hA, X_H1, None)
            with pe.Fori(1, NB) as b:
                pe.wait_ge(gated_ready, FC * b + FC)
                hidden(b, hA, X_H1, FC * b - (FC - 1))
            with pe.Fori(0, NB) as b:
                pe.wait_ge(gelu_ready, FC * b + FC)
                hidden(b, hB, X_H2, FC * b + (FC * NB - (FC - 1)))

            def project_y(b):
                pe.wait_ge(gelu_ready, FC * NB + FC * (b + 1))
                if b >= 2:
                    pe.wait_ge(yT_ready, b - 1)
                for k in range(FC):
                    last = mm(PS[:, b % 2, :], tw[:, X_W3 + D * k:X_W3 + D * (k + 1)], hA[:, k, tokens(b)],
                              start=k == 0, stop=k == FC - 1)
                last.then_inc(y_psum, 1)

            project_y(0)
            for b in range(NB):
                if b + 1 < NB:
                    project_y(b + 1)
                pe.wait_ge(yT_ready, b + 1)
                if b >= 2:
                    pe.wait_ge(y_drained, b - 1)
                transpose_tiles(2 + b % 2, yT[:, b % 2, :].rearrange("p (t n) -> p t n", n=P)).then_inc(y_tokens, 1)


def setup_pack(i):
    a = {k[len("L0_attn_"):]: np.asarray(v) for k, v in i.items() if k.startswith("L0_attn_")}
    R = D // 2
    pack = np.zeros((P, SETUP_COLS), np.float32)

    def swapped(w):
        return w.reshape(w.shape[:-1] + (D // 2, 2))[..., ::-1].reshape(w.shape)

    pack[:, W_D:W_D + R], pack[:, W_D + R:W_D + D] = a["Wd_q_w"], a["Wd_kv_w"]
    pack[:R, W_QC:W_QC + D] = a["Wu_q_w"]
    pack[:R, W_QR:W_QR + D] = a["Wq_r_w"]
    pack[:R, W_QS:W_QS + D] = swapped(a["Wq_r_w"])
    pack[R:, W_KC:W_KC + D] = a["Wu_k_w"]
    pack[:, W_KR:W_KR + D] = a["Wk_r_w"]
    pack[:, W_KS:W_KS + D] = swapped(a["Wk_r_w"])
    pack[R:, W_V:W_V + D] = a["Wu_v_w"]
    pack[:, B_V:B_V + D] = a["Wu_v_b"]
    for h in range(H):
        pack[HD * h:HD * (h + 1), SEL + h] = 1
    pack[:R, BIAS], pack[R:, BIAS] = a["Wd_q_b"], a["Wd_kv_b"]
    for n, b in enumerate((a["Wu_q_b"], a["Wq_r_b"], swapped(a["Wq_r_b"]),
                           a["Wu_k_b"], a["Wk_r_b"], swapped(a["Wk_r_b"]))):
        pack[:, BIAS + 1 + n] = b
    return pack


def tail_pack(i):
    f = {k[len("L0_ffn_"):]: np.asarray(v) for k, v in i.items() if k.startswith("L0_ffn_")}
    pack = np.zeros((P, TAIL_COLS), np.float32)
    pack[:, X_W1:X_W1 + F], pack[:, X_W2:X_W2 + F] = f["w1_w"].T, f["w2_w"].T
    for k in range(FC):
        pack[:, X_H1 + F * k:X_H1 + F * (k + 1)] = f["h1_w"].T[P * k:P * (k + 1)]
        pack[:, X_H2 + F * k:X_H2 + F * (k + 1)] = f["h2_w"].T[P * k:P * (k + 1)]
        pack[:, X_W3 + D * k:X_W3 + D * (k + 1)] = f["w3_w"].T[P * k:P * (k + 1)]
    wo = np.asarray(i["L0_attn_Wo_w"])
    for g in range(NG):
        for j in range(GH):
            r = HD * (GH * g + j)
            pack[32 * j:32 * j + HD, X_WO + D * g:X_WO + D * (g + 1)] = wo[r:r + HD]
    pack[:, X_BO:X_BO + D] = np.asarray(i["L0_attn_Wo_b"])
    for n, name in enumerate(("w1_s", "w2_s", "h1_s", "h2_s")):
        pack[:, X_S + FC * n:X_S + FC * (n + 1)] = f[name].reshape(FC, P).T
    pack[:, X_S + 4 * FC] = f["w3_s"]
    return pack


def rotation_tables():
    pos = np.arange(T, dtype=np.float32)
    ids = np.arange(D // 2, dtype=np.float32)
    theta = (np.float32(10000.0) ** (np.float32(-2.0) * ids)).astype(np.float32) / np.float32(D // 2)
    angle = theta[:, None] * pos[None, :]
    cos = np.repeat(np.cos(angle), 2, axis=0).astype(np.float32)
    sin = np.repeat(np.sin(angle), 2, axis=0).astype(np.float32)
    sin[0::2] = -sin[0::2]
    return cos, sin


def kernel(**inputs):
    import concourse.bacc as bacc
    from concourse.bass_utils import run_bass_kernel_spmd

    cos, sin = rotation_tables()
    arrays = {
        "x": np.ascontiguousarray(np.asarray(inputs["L0_attn_x"])[0]),
        "setup": setup_pack(inputs),
        "tail": tail_pack(inputs),
        "cos": cos,
        "sin": sin,
        "identity": np.eye(P, dtype=np.float32),
    }
    nc = bacc.Bacc("TRN2", target_bir_lowering=False, num_devices=1)
    fp32 = mybir.dt.float32
    args = [nc.dram_tensor(name, a.shape, fp32, kind="ExternalInput").ap() for name, a in arrays.items()]
    for name in ("q_scratch", "k_scratch"):
        args.append(nc.dram_tensor(name, (D, SPLIT, T), mybir.dt.bfloat16, kind="Internal").ap())
    args.append(nc.dram_tensor("out", (T, D), fp32, kind="ExternalOutput").ap())
    layer(nc, *args)
    result = run_bass_kernel_spmd(nc, [arrays], core_ids=[0])
    return result.results[0]["out"].reshape(1, T, D)
```

```python
from contextlib import ExitStack

import concourse.bass as bass
from concourse import mybir
import numpy as np

T, D, H, HD, F = 2048, 128, 16, 8, 512
P = 128
BLK = 512
NB = T // BLK
NT = T // P
TPB = BLK // P
NG, GH = 4, 4
NI = NG * NB
VW = HD + 1
FC = F // P
SPLIT = 3
ROWS = SPLIT * SPLIT * HD
EPS = 1e-5
INEXACT = 0.5
SCORE_SCALE = 1.0 / 12.0
SAFE_SCORE = 60.0
SAFE_PRODUCT = 0.98 * (SAFE_SCORE / SCORE_SCALE) ** 2

ONE_PAIR = float(np.array([0x3F803F80], np.uint32).view(np.float32)[0])

(W_D, W_QC, W_QR, W_QS, W_KC, W_KR, W_KS, W_V, B_V) = (D * n for n in range(9))
SEL = 9 * D
BIAS = SEL + H
SETUP_COLS = BIAS + 7
X_W1, X_W2 = 0, F
X_H1, X_H2 = 2 * F, 2 * F + FC * F
X_W3 = 2 * F + 2 * FC * F
FFN_COLS = X_W3 + FC * D
X_WO = 0
X_BO = X_WO + D
X_S = X_BO + D
REST_COLS = X_S + 4 * FC + 1
WARM_START, WARM_FLAG = 16, 8
EARLY = NI - NB + 1


class Steps:

    def __init__(self, engine, sem):
        self.engine, self.sem, self.n = engine, sem, 0

    def mark(self, instruction):
        instruction.then_inc(self.sem, 1)
        self.n += 1
        return self.n

    def then_wait(self, instruction):
        self.engine.wait_ge(self.sem, self.mark(instruction))


def layer(nc, x_dram, setup_dram, ffn_dram, rest_dram, cos_dram, sin_dram, ident_dram, q_scratch, k_scratch, out):
    fp32, fp32r, bf16, int32 = mybir.dt.float32, mybir.dt.float32r, mybir.dt.bfloat16, mybir.dt.int32
    ALU, ACT, AX = mybir.AluOpType, mybir.ActivationFunctionType, mybir.AxisListType
    ctx = ExitStack()
    with ctx:
        size = {fp32: 4, fp32r: 4, bf16: 2, int32: 4}
        top = [-(-nc.sbuf_base // 32) * 32]

        def over(name, shape, dt, at):
            return nc.alloc_sbuf_tensor_at(name, shape, dt, offset=at)

        def sb(name, shape, dt=fp32):
            at = top[0]
            top[0] += -(-int(np.prod(shape[1:])) * size[dt] // 32) * 32
            return over(name, shape, dt, at)

        def sem(name):
            return ctx.enter_context(nc.semaphore(name))

        at_QT = top[0]
        QT = sb("q_operand", [P, NI, GH, BLK], bf16)
        at_KT = top[0]
        KT = sb("k_operand", [P, NG, GH, T], bf16)
        at_probs = top[0]
        probs = sb("probs", [P, 4, GH, BLK])
        at_split = top[0]
        Ks = sb("k_split", [P, SPLIT, T], bf16)
        Qs = sb("q_split", [P, SPLIT, T], bf16)
        at_V = top[0]
        V = sb("v_all", [P, NT, NG, GH * VW])
        Vst = sb("v_group", [P, NT, GH * VW])
        attn = sb("attn", [P, NB, BLK // 32, NG * HD])
        ident = sb("ident", [P, P])
        ident_bf = sb("ident_bf", [P, P], bf16)
        oT = sb("o_tokens", [P, BLK // 32, 32])
        rden = sb("rden", [P, BLK // 32, 1])
        stats = sb("stats", [P, NB, TPB, 6])
        mv = sb("mean_var", [P, NB, TPB, 2])
        rstd = sb("rstd", [P, NB, TPB])
        minus_half = sb("minus_half", [P, TPB])
        norm_max = sb("norm_max", [H, 2 * NB])
        side_max = sb("side_max", [H, 2])
        norm_prod = sb("norm_prod", [H, 1])
        bound = sb("bound", [1, 1])
        unsafe = sb("unsafe", [1, 1], int32)
        half_max = sb("half_max", [P, GH * TPB, 2])
        neg_max = sb("neg_max", [P, GH * TPB])
        neg_rest = sb("neg_rest", [P, GH * TPB])
        shift_cols = sb("shift_cols", [P, P], bf16)
        shift_rows = sb("shift_rows", [P, P], bf16)
        ones = sb("ones", [P, 1])
        low_range = sb("low_range", [P, 2, 4])
        low_nonzero = sb("low_nonzero", [P, 1])
        inexact = sb("inexact", [1, 1], int32)
        assert top[0] <= nc.sbuf_usable_end
        shift_parts = shift_cols[:, 0:SPLIT * GH * TPB].rearrange("p (s q) -> p s q", s=SPLIT)

        PS = ctx.enter_context(nc.psum_tensor("psum", [P, 8, BLK], fp32))
        UNITS = 3
        ACC, MISC = 6, 7

        probs_f = probs[:, :, :, :].rearrange("p a b c -> p (a b c)")
        xs = probs_f[:, 0:T].rearrange("p (t d) -> p t d", d=D)
        xnT = probs_f[:, T:2 * T]
        ct = probs_f[:, 2 * T:3 * T]
        squares = probs_f[:, 3 * T:4 * T].bitcast(bf16).rearrange("p (s t) -> p s t", s=2)
        KT_f = KT[:, :, :, :].rearrange("p g j n -> p (g j n)").bitcast(fp32)
        QT_f = QT[:, :, :, :].rearrange("p i j n -> p (i j n)").bitcast(fp32)
        cosT, sinT = KT_f[:, 3 * 4096:3 * 4096 + T], KT_f[:, 3 * 4096 + T:4 * 4096]
        wp = KT_f[:, 2 * 4096:2 * 4096 + SETUP_COLS]
        tmp = QT_f[:, 3 * 4096:4 * 4096].rearrange("p (s k n) -> p s k n", s=2, n=BLK)
        sel_bf = QT_f[:, 2 * 4096:2 * 4096 + H // 2].bitcast(bf16)

        warm = oT[:, :, :].rearrange("p b d -> p (b d)")[:, 0:BLK // 2].bitcast(bf16)

        PER_I, PER_G = GH * BLK * 2, GH * T * 2
        w_raw = over("w_raw", [P, FFN_COLS], fp32, at_split)
        w_hi = over("w_hi", [P, FFN_COLS], fp32r, at_QT)
        w_lo = over("w_lo", [P, FFN_COLS], fp32r, at_QT + 4 * FFN_COLS)
        W_FREE = -(-8 * FFN_COLS // PER_I)
        rest_t = over("rest", [P, REST_COLS], fp32, at_QT + PER_I * W_FREE)
        rest = rest_t[:, :]
        xr = over("x_residual", [P, 2, TPB, D], fp32, at_QT + PER_I * (W_FREE + 1))
        yT = over("y_T", [P, 2, BLK], fp32, at_QT + PER_I * (W_FREE + 2))
        assert W_FREE == 11 and 4 * REST_COLS <= PER_I
        h_hi = [over(f"h_hi{b}", [P, FC, BLK], fp32r, at_KT + PER_G * b) for b in range(NB)]
        h_lo = [over(f"h_lo{b}", [P, FC, BLK], fp32r, at_KT + PER_G * b + PER_G // 2) for b in range(NB)]
        h2_hi = [over(f"h2_hi{s}", [P, FC, BLK], fp32r, at_probs + PER_G * s) for s in range(2)]
        h2_lo = [over(f"h2_lo{s}", [P, FC, BLK], fp32r, at_probs + PER_G * s + PER_G // 2) for s in range(2)]
        oTn = over("attn_T", [P, BLK], fp32, at_KT + PER_G * 2)
        xT_hi = over("xT_hi", [P, T], fp32r, at_split)
        xT_lo = over("xT_lo", [P, T], fp32r, at_split + 4 * T)
        ao = over("attn_out", [P, TPB, D], fp32, at_split + 8 * T)
        ln = over("ln", [P, TPB, D], fp32, at_split + 8 * T + 4 * BLK)
        ln2 = over("ln2", [P, TPB, D], fp32, at_split + 8 * T + 8 * BLK)
        silu = over("silu", [P, 2, BLK], fp32, at_V)
        act_f = over("activation", [P, 2, BLK], fp32, at_V + 8 * BLK)

        def x1(b):
            return attn[:, b, :, :].rearrange("p t d -> p (t d)").rearrange("p (t d) -> p t d", d=D)

        x_loaded = [sem(f"x_loaded{b}") for b in range(NB)]
        tables_loaded = [sem(f"tables_loaded{b}") for b in range(NB)]
        weights_loaded, ident_loaded = sem("weights_loaded"), sem("ident_loaded")
        ffn_loaded, rest_loaded = sem("ffn_loaded"), sem("rest_loaded")
        x_again = [sem(f"x_again{s}") for s in range(2)]
        stored = sem("stored")
        operands_in = sem("operands_in")
        dve = sem("dve_steps")
        pool = sem("pool_steps")
        pool_constants, dve_constants = sem("pool_constants"), sem("dve_constants")
        var_ready, rstd_ready, xn_ready = sem("var_ready"), sem("rstd_ready"), sem("xn_ready")
        xnT_psum, xnT_ready, ct_psum, ct_ready = sem("xnT_psum"), sem("xnT_ready"), sem("ct_psum"), sem("ct_ready")
        side_psum, side_drained, side_ready = sem("side_psum"), sem("side_drained"), sem("side_ready")
        v_psum, v_drained = sem("v_psum"), sem("v_drained")
        high_ready, squares_ready = sem("high_ready"), sem("squares_ready")
        rest_ready, mid_ready, low_ready = sem("rest_ready"), sem("mid_ready"), sem("low_ready")
        norm_psum, norm_reduced = sem("norm_psum"), sem("norm_reduced")
        product_ready, product_psum, flag_ready = sem("product_ready"), sem("product_psum"), sem("flag_ready")
        k_pads, q_pads = sem("k_pads"), sem("q_pads")
        max_scores, max_reduced, max_steps = sem("max_scores"), sem("max_reduced"), sem("max_steps")
        shift_split, shift_psum, shift_rows_ready, shift_in = (
            sem("shift_split"), sem("shift_psum"), sem("shift_rows_ready"), sem("shift_in"))
        scores_ready, probs_ready, probs_used = sem("scores_ready"), sem("probs_ready"), sem("probs_used")
        v_staged, acc_free, attn_steps = sem("v_staged"), sem("acc_free"), sem("attn_steps")
        w_split = sem("w_split")
        low_any, inexact_psum, inexact_ready = sem("low_any"), sem("inexact_psum"), sem("inexact_ready")
        oTn_ready = sem("oTn_ready")
        proj_psum, proj_drained, x1_ready, ln2_ready = (
            sem("proj_psum"), sem("proj_drained"), sem("x1_ready"), sem("ln2_ready"))
        tail_var, tail_rstd = sem("tail_var"), sem("tail_rstd")
        xT_psum, xT_ready = sem("xT_psum"), sem("xT_ready")
        gate_psum, silu_ready, gated_ready = sem("gate_psum"), sem("silu_ready"), sem("gated_ready")
        hidden_psum, gelu_ready = sem("hidden_psum"), sem("gelu_ready")
        h_high = sem("h_high")
        g_low, h_low = sem("g_low"), sem("h_low")
        y_psum, yT_ready, y_tokens, y_drained, y_ready = (
            sem("y_psum"), sem("yT_ready"), sem("y_tokens"), sem("y_drained"), sem("y_ready"))
        out_done = sem("out_done")

        def tokens(b):
            return slice(b * BLK, (b + 1) * BLK)

        def tiles(b):
            return slice(b * TPB, (b + 1) * TPB)

        K_DMAS, Q_DMAS = SPLIT * SPLIT, SPLIT

        def operands_of(i):
            return 16 * (K_DMAS + NB * Q_DMAS) * (i // NB) + 16 * Q_DMAS * (i % NB) + 16 * (K_DMAS + Q_DMAS)

        STAGES = ("B0", "B1", "C0", "B2", "C1", "Y0", "B3", "Z0", "C2", "Y1", "C3", "Z1", "Y2", "Z2", "Y3", "Z3")
        HIDDEN = [s for s in STAGES if s[0] in "BC"]

        def hidden_src(stage):
            b = int(stage[1])
            return (h_hi[b], h_lo[b]) if stage[0] != "C" else (h2_hi[b % 2], h2_lo[b % 2])

        def hidden_dst(stage):
            b = int(stage[1])
            return (h_hi[b], h_lo[b]) if stage[0] == "C" else (h2_hi[b % 2], h2_lo[b % 2])

        def parts_of(stage):
            b = int(stage[1])
            if stage[0] == "B":
                return g_low, FC * (b + 1)
            before = {"C": "B", "Y": "C"}[stage[0]] + stage[1]
            return h_low, FC * (HIDDEN.index(before) + 1)

        ROOTS_BEFORE = {1: 2 * NB - 2, 3: 2 * NB - 1}

        NORMS_AFTER = ((0, 1), (2, 3), (4, 5), (6, 7))

        def side_banks(m):
            return (0, 1, 2) if m % 2 == 0 else (3, 4, 5)

        def norm_bank(m):
            return MISC if m % 2 == 0 else ACC

        scores = PS[:, 0:2 * UNITS, :].rearrange("p b n -> p (b n)")

        def unit(engine, u):
            return scores[:, 2 * BLK * u:2 * BLK * (u + 1)] if isinstance(u, int) else \
                scores[:, bass.ds(u * (2 * BLK), 2 * BLK)]

        block = ctx.enter_context(nc.Block())

        @block.sync
        def _(sp):
            for b in range(NB):
                sp.dma_start(xs[:, tiles(b), :],
                             x_dram[tokens(b), :].rearrange("(t p) d -> p t d", p=P)).then_inc(x_loaded[b], 16)
            for b in range(NB):
                sp.dma_start(cosT[:, tokens(b)], cos_dram[:, tokens(b)]).then_inc(tables_loaded[b], 16)
                sp.dma_start(sinT[:, tokens(b)], sin_dram[:, tokens(b)]).then_inc(tables_loaded[b], 16)

            k_rows = k_scratch.rearrange("(g j d) a n -> g d a j n", g=NG, d=HD)
            q_rows = q_scratch.rearrange("(g j d) b n -> g (d b) j n", g=NG, d=HD)

            def lay_out_k(g, cols):
                for a in range(SPLIT):
                    for b in range(SPLIT):
                        r = SPLIT * HD * a + b
                        sp.dma_start(KT[r:r + SPLIT * HD - 2:SPLIT, g, :, cols],
                                     k_rows[g, :, a, :, cols]).then_inc(operands_in, 16)

            def lay_out_q(g, blk):
                for a in range(SPLIT):
                    r = SPLIT * HD * a
                    sp.dma_start(QT[r:r + SPLIT * HD, NB * g + blk, :, :],
                                 q_rows[g, :, :, tokens(blk)]).then_inc(operands_in, 16)

            sp.wait_ge(k_pads, 1)
            sp.wait_ge(q_pads, 1)
            for m in range(2 * NB):
                part, scratch, b = (Ks, k_scratch, m) if m < NB else (Qs, q_scratch, m - NB)
                sp.wait_ge(low_ready, m + 1)
                sp.dma_start(scratch[:, :, tokens(b)], part[:, :, tokens(b)]).then_inc(stored, 16)
                if m >= NB - 1:
                    sp.wait_ge(stored, 16 * (m + 1))
                if m == NB - 1:
                    lay_out_k(0, slice(0, T))
                elif m >= NB:
                    if b:
                        sp.wait_ge(operands_in, operands_of(b - 1))
                    lay_out_q(0, b)
            for g in range(1, NG):
                sp.wait_ge(k_pads, g + 1)
                sp.wait_ge(q_pads, g + 1)
                for b in range(NB):
                    sp.wait_ge(operands_in, operands_of(NB * g + b - 1))
                    if b == 0:
                        lay_out_k(g, slice(0, T))
                    lay_out_q(g, b)

            sp.wait_ge(flag_ready, 1)
            general = sp.value_load(unsafe[0:1, 0:1], min_val=0, max_val=1)
            with sp.If(general > 0):
                with sp.Fori(0, NI) as i:
                    sp.wait_ge(shift_rows_ready, i + 2)
                    for s in range(SPLIT):
                        n = GH * TPB
                        sp.dma_start(QT[ROWS + s:ROWS + s + 1, i, :, :].rearrange("p j n -> p (j n)"),
                                     shift_rows[n * s:n * s + n, :]).then_inc(shift_in, 16)

            sp.wait_ge(operands_in, operands_of(NI - 1))
            sp.dma_start(w_raw[:, :], ffn_dram[:, :]).then_inc(ffn_loaded, 16)
            sp.wait_ge(probs_used, NT * (W_FREE + 1))
            sp.dma_start(rest, rest_dram[:, :]).then_inc(rest_loaded, 16)
            sp.wait_ge(probs_used, NT * (W_FREE + 2))
            for b in range(NB):
                if b >= 2:
                    sp.wait_ge(x1_ready, b - 1)
                sp.dma_start(xr[:, b % 2, :, :], x_dram[tokens(b), :].rearrange("(t p) d -> p t d", p=P)
                             ).then_inc(x_again[b % 2], 16)
            for b in range(NB):
                sp.wait_ge(y_ready, b + 1)
                sp.dma_start(out[tokens(b), :].rearrange("(t p) d -> p t d", p=P), x1(b)).then_inc(out_done, 16)
            sp.wait_ge(out_done, 16 * NB)

        @block.gpsimd
        def _(gp):
            steps = Steps(gp, pool)
            k_pad = KT_f[64:P, :].rearrange("p (g n) -> p g n", g=NG)
            q_pad = QT_f[64:P, :].rearrange("p (g n) -> p g n", g=NG)
            nc.gpsimd.memset(warm[:, :], 0.0).then_inc(pool_constants, 1)
            nc.gpsimd.memset(ones[:, :], 1.0)
            nc.gpsimd.memset(minus_half[:, :], -0.5).then_inc(pool_constants, 1)
            gp.wait_ge(pool_constants, 2)

            def root(var, out_rstd, ready):
                steps.then_wait(nc.gpsimd.tensor_scalar(out_rstd, var, EPS, None, ALU.add))
                nc.gpsimd.tensor_tensor(out_rstd, out_rstd, minus_half[:, :], ALU.pow).then_inc(ready, 1)

            for b in range(NB):
                gp.wait_ge(var_ready, b + 1)
                root(mv[:, b, :, 1], rstd[:, b, :], rstd_ready)
            nc.gpsimd.memset(V[:, :, :, :].rearrange("p t g (j w) -> p (t g j) w", w=VW)[:, :, HD:VW],
                             1.0).then_inc(pool_constants, 1)
            gp.wait_ge(pool_constants, 3)
            nc.gpsimd.memset(k_pad[:, 0, :], ONE_PAIR).then_inc(k_pads, 1)
            gp.wait_ge(k_pads, 1)

            def low(m):
                part, b = (Ks, m) if m < NB else (Qs, m - NB)
                gp.wait_ge(mid_ready, m + 1)
                nc.gpsimd.tensor_tensor(part[:, 2, tokens(b)], tmp[:, m % 2, 3, :], part[:, 1, tokens(b)],
                                        ALU.subtract).then_inc(low_ready, 1)

            for m in range(2 * NB):
                part, b = (Ks, m) if m < NB else (Qs, m - NB)
                gp.wait_ge(high_ready, m + 1)
                if m >= 2:
                    gp.wait_ge(low_ready, m - 1)
                nc.gpsimd.tensor_tensor(tmp[:, m % 2, 3, :], tmp[:, m % 2, 2, :], part[:, 0, tokens(b)],
                                        ALU.subtract).then_inc(rest_ready, 1)
                if m:
                    low(m - 1)
            low(2 * NB - 1)

            def stage_v(g, half):
                t = slice(half * NT // 2, (half + 1) * NT // 2)
                nc.gpsimd.tensor_copy(Vst[:, t, :], V[:, t, g, :]).then_inc(v_staged, 1)

            gp.wait_ge(v_drained, NB)
            stage_v(0, 0)
            stage_v(0, 1)
            gp.wait_ge(v_staged, 2)
            gp.wait_ge(low_ready, 2 * NB)
            gp.wait_ge(squares_ready, 2 * NB)
            gp.wait_ge(side_ready, 2 * NB)
            gp.wait_ge(norm_psum, 2 * NB)
            for g in range(1, NG):
                nc.gpsimd.memset(k_pad[:, g, :], ONE_PAIR).then_inc(k_pads, 1)
                gp.wait_ge(k_pads, g + 1)
                nc.gpsimd.memset(q_pad[:, g, :], 0.0).then_inc(q_pads, 1)
                gp.wait_ge(q_pads, g + 1)
            with gp.Fori(1, NG) as g:
                gp.wait_ge(probs_used, NG * NT * g - NT // 2)
                stage_v(g, 0)
                gp.wait_ge(probs_used, NG * NT * g)
                stage_v(g, 1)


            def tail_root(n):
                gp.wait_ge(tail_var, n + 1)
                root(mv[:, n % NB, :, 1], rstd[:, n % NB, :], tail_rstd)

            for n in range(2 * (NB - 1)):
                tail_root(n)
            for n in range(FC * NB):
                if n in ROOTS_BEFORE:
                    tail_root(ROOTS_BEFORE[n])
                b, c = divmod(n, FC)
                gp.wait_ge(h_high, n + 1)
                nc.gpsimd.tensor_tensor(h_lo[b][:, c, :], act_f[:, n % 2, :], h_hi[b][:, c, :].bitcast(fp32),
                                        ALU.subtract).then_inc(g_low, 1)
            for b in range(NB):
                tail_root(2 * NB + b)

        @block.scalar
        def _(act):
            act.dma_start(wp, setup_dram[:, :]).then_inc(weights_loaded, 16)
            act.dma_start(ident[:, :], ident_dram[:, :]).then_inc(ident_loaded, 16)
            act.wait_ge(weights_loaded, 16)

            def drain_xnT(b):
                act.wait_ge(xnT_psum, b + 1)
                nc.scalar.activation(xnT[:, tokens(b)], PS[:, MISC, :], ACT.Copy).then_inc(xnT_ready, 1)

            def drain_ct(b):
                act.wait_ge(ct_psum, b + 1)
                nc.scalar.activation(ct[:, tokens(b)], PS[:, ACC, :], ACT.Identity,
                                     bias=wp[:, BIAS:BIAS + 1]).then_inc(ct_ready, 1)

            def mid(m):
                part, b = (Ks, m) if m < NB else (Qs, m - NB)
                act.wait_ge(rest_ready, m + 1)
                nc.scalar.activation(part[:, 1, tokens(b)], tmp[:, m % 2, 3, :], ACT.Copy).then_inc(mid_ready, 1)

            drain_xnT(0)
            drain_ct(0)
            drain_xnT(1)
            drain_ct(1)
            for m in range(2 * NB):
                part, b = (Ks, m) if m < NB else (Qs, m - NB)
                act.wait_ge(side_ready, m + 1)
                nc.scalar.activation(part[:, 0, tokens(b)], tmp[:, m % 2, 2, :], ACT.Copy).then_inc(high_ready, 1)
                nc.scalar.activation(squares[:, m // NB, tokens(b)], tmp[:, m % 2, 2, :],
                                     ACT.Square).then_inc(squares_ready, 1)
                if m + 2 < NB:
                    drain_xnT(m + 2)
                    drain_ct(m + 2)
                if m:
                    mid(m - 1)
            mid(2 * NB - 1)

            act.wait_ge(norm_psum, 2 * NB)

            def exps(i, t, first=False):
                if not first:
                    act.wait_ge(probs_used, NT * i + (t - 3))
                for half in range(2):
                    act.wait_ge(scores_ready, 2 * NT * i + (2 * t + half + 1))
                    u = (2 * NT * i + (2 * t + half)) % UNITS
                    nc.scalar.activation(probs[:, t % 4, 2 * half:2 * half + 2, :].rearrange("p j n -> p (j n)"),
                                         unit(act, u), ACT.Exp, scale=SCORE_SCALE).then_inc(probs_ready, 1)

            for t in range(4):
                exps(0, t, True)
            for t in range(4, NT):
                exps(0, t)
            with act.Fori(1, NI) as i:
                for t in range(NT):
                    exps(i, t)

            def gated_high(n):
                b, c = divmod(n, FC)
                act.wait_ge(gated_ready, n + 1)
                nc.scalar.activation(h_hi[b][:, c, :], act_f[:, n % 2, :], ACT.Copy).then_inc(h_high, 1)

            act.wait_ge(rest_loaded, 16)
            for n in range(FC * NB):
                c, slot = n % FC, n % 2
                act.wait_ge(gate_psum, 2 * n + 1)
                if n >= 2:
                    act.wait_ge(gated_ready, n - 1)
                nc.scalar.activation(silu[:, slot, :], PS[:, slot, :], ACT.Silu,
                                     scale=rest[:, X_S + c:X_S + c + 1]).then_inc(silu_ready, 1)
                if n:
                    gated_high(n - 1)
            gated_high(FC * NB - 1)
            n = 0
            for stage in STAGES:
                b = int(stage[1])
                if stage[0] in "BC":
                    col = X_S + (2 if stage[0] == "B" else 3) * FC
                    for c in range(FC):
                        act.wait_ge(hidden_psum, n + 1)
                        if n >= 2:
                            act.wait_ge(h_low, n - 1)
                        else:
                            act.wait_ge(g_low, FC * NB - 1 + n)
                        nc.scalar.activation(act_f[:, n % 2, :], PS[:, 4 + n % 2, :], ACT.Gelu,
                                             scale=rest[:, col + c:col + c + 1]).then_inc(gelu_ready, 1)
                        act.wait_ge(gelu_ready, n + 1)
                        nc.scalar.activation(hidden_dst(stage)[0][:, c, :], act_f[:, n % 2, :],
                                             ACT.Copy).then_inc(h_high, 1)
                        n += 1
                elif stage[0] == "Y":
                    act.wait_ge(y_psum, b + 1)
                    if b >= 2:
                        act.wait_ge(y_tokens, b - 1)
                    nc.scalar.activation(yT[:, b % 2, :], PS[:, b % 2, :], ACT.Copy,
                                         scale=rest[:, X_S + 4 * FC:X_S + 4 * FC + 1]).then_inc(yT_ready, 1)

        @block.vector
        def _(ve):
            steps = Steps(ve, dve)
            q_pad = QT_f[64:P, :].rearrange("p (g n) -> p g n", g=NG)
            for b in range(NB):
                ve.wait_ge(x_loaded[b], 16)
                for t in range(TPB):
                    last = nc.vector.bn_stats(stats[:, b, t, :], xs[:, TPB * b + t, :])
                steps.then_wait(last)
                for t in range(TPB):
                    last = nc.vector.bn_aggr(mv[:, b, t, :], stats[:, b, t, :])
                last.then_inc(var_ready, 1)

            def normalise(b):
                ve.wait_ge(rstd_ready, b + 1)
                for t in range(TPB):
                    last = nc.vector.tensor_scalar(xs[:, TPB * b + t, :], xs[:, TPB * b + t, :], mv[:, b, t, 0:1],
                                                   rstd[:, b, t:t + 1], ALU.subtract, ALU.mult)
                last.then_inc(xn_ready, 1)

            def side(m):
                b, bias = (m, BIAS + 4) if m < NB else (m - NB, BIAS + 1)
                content, rotated, swapped = side_banks(m)
                t1, t2, whole = (tmp[:, m % 2, k, :] for k in range(3))
                ve.wait_ge(side_psum, m + 1)
                steps.mark(nc.vector.scalar_tensor_tensor(t1, PS[:, rotated, :], wp[:, bias + 1:bias + 2],
                                                          cosT[:, tokens(b)], ALU.add, ALU.mult))
                nc.vector.scalar_tensor_tensor(t2, PS[:, swapped, :], wp[:, bias + 2:bias + 3],
                                               sinT[:, tokens(b)], ALU.add, ALU.mult)
                ve.wait_ge(dve, steps.n)
                nc.vector.scalar_tensor_tensor(t1, PS[:, content, :], wp[:, bias:bias + 1], t1,
                                               ALU.add, ALU.add).then_inc(side_drained, 1)
                ve.wait_ge(side_drained, m + 1)
                if m >= 2:
                    ve.wait_ge(squares_ready, m - 1)
                    ve.wait_ge(rest_ready, m - 1)
                nc.vector.tensor_tensor(whole, t1, t2, ALU.add).then_inc(side_ready, 1)

            def values(b):
                ve.wait_ge(v_psum, b + 1)
                if b == 0:
                    ve.wait_ge(pool_constants, 3)
                for t in range(TPB):
                    last = nc.vector.tensor_tensor(
                        V[:, TPB * b + t, :, :].rearrange("p g (j w) -> p (g j) w", w=VW)[:, :, 0:HD],
                        PS[:, MISC, D * t:D * (t + 1)].rearrange("p (h d) -> p h d", d=HD),
                        wp[:, B_V:B_V + D].rearrange("p (h d) -> p h d", d=HD), ALU.add)
                last.then_inc(v_drained, 1)

            normalise(0)
            ve.wait_ge(ident_loaded, 16)
            nc.vector.tensor_copy(ident_bf[:, :], ident[:, :]).then_inc(dve_constants, 1)
            normalise(1)
            ve.wait_ge(weights_loaded, 16)
            nc.vector.tensor_copy(sel_bf, wp[:, SEL:SEL + H]).then_inc(dve_constants, 1)
            normalise(2)
            normalise(3)
            nc.vector.memset(q_pad[:, 0, :], 0.0).then_inc(q_pads, 1)

            def reduce_norm(m):
                ve.wait_ge(norm_psum, m + 1)
                nc.vector.reduce_max(norm_max[:, m:m + 1], PS[0:H, norm_bank(m), :], AX.X).then_inc(norm_reduced, 1)

            for b in range(NB):
                ve.wait_ge(tables_loaded[b], 32)
                side(b)
                values(b)
            for b in range(NB):
                side(NB + b)
                for m in NORMS_AFTER[b]:
                    reduce_norm(m)

            ve.wait_ge(norm_reduced, 2 * NB)
            steps.then_wait(nc.vector.reduce_max(side_max[:, :], norm_max[:, :].rearrange("h (s b) -> h s b", s=2), AX.X))
            nc.vector.tensor_tensor(norm_prod[:, :], side_max[:, 0:1], side_max[:, 1:2],
                                    ALU.mult).then_inc(product_ready, 1)
            nc.vector.memset(PS[:, ACC, :], 0.0).then_inc(acc_free, 1)
            ve.wait_ge(product_psum, 1)
            steps.then_wait(nc.vector.reduce_max(bound[:, :], PS[0:1, 0, 0:H], AX.X))
            nc.vector.tensor_scalar(unsafe[:, :], bound[:, :], SAFE_PRODUCT, None, ALU.is_gt).then_inc(flag_ready, 1)
            ve.wait_ge(flag_ready, 1)
            general = ve.value_load(unsafe[0:1, 0:1], min_val=0, max_val=1)
            with ve.If(general > 0):
                nq = GH * TPB
                nc.vector.memset(shift_cols[:, :], 0.0).then_inc(shift_rows_ready, 1)
                ve.wait_ge(shift_rows_ready, 1)
                with ve.Fori(0, NI) as i:
                    for u in range(2 * nq):
                        ve.wait_ge(max_scores, 2 * nq * i + (u + 1))
                        h = u % 2
                        nc.vector.tensor_reduce(half_max[:, u // 2, h:h + 1], PS[:, 2 * h:2 * h + 2, :], AX.XY,
                                                ALU.max, negate=True).then_inc(max_reduced, 1)
                    ve.wait_ge(max_reduced, 2 * nq * i + 2 * nq)
                    nc.vector.tensor_tensor(neg_max[:, :], half_max[:, :, 0], half_max[:, :, 1],
                                            ALU.min).then_inc(max_steps, 1)
                    ve.wait_ge(max_steps, 5 * i + 1)
                    nc.vector.tensor_copy(shift_parts[:, 0, :], neg_max[:, :]).then_inc(max_steps, 1)
                    ve.wait_ge(max_steps, 5 * i + 2)
                    nc.vector.tensor_tensor(neg_rest[:, :], neg_max[:, :], shift_parts[:, 0, :],
                                            ALU.subtract).then_inc(max_steps, 1)
                    ve.wait_ge(max_steps, 5 * i + 3)
                    nc.vector.tensor_copy(shift_parts[:, 1, :], neg_rest[:, :]).then_inc(max_steps, 1)
                    ve.wait_ge(max_steps, 5 * i + 4)
                    nc.vector.tensor_tensor(shift_parts[:, 2, :], neg_rest[:, :], shift_parts[:, 1, :],
                                            ALU.subtract).then_inc(max_steps, 1)
                    ve.wait_ge(shift_psum, i + 1)
                    nc.vector.tensor_copy(shift_rows[:, :], PS[:, MISC, 0:P // 2].bitcast(bf16)
                                          ).then_inc(shift_rows_ready, 1)
                    ve.wait_ge(shift_in, 16 * SPLIT * i + 16 * SPLIT)

            def drain_attention(i):
                ve.wait_ge(probs_used, NT * i + NT)
                nc.vector.transpose(oT[:, :, :].rearrange("p b d -> p (b d)"), PS[:, ACC, :]).then_inc(acc_free, 1)
                ve.wait_ge(acc_free, i + 2)
                nc.vector.reciprocal(rden[:, :, :], oT[:, :, HD:VW]).then_inc(attn_steps, 1)
                ve.wait_ge(attn_steps, 2 * i + 1)
                nc.vector.tensor_tensor(attn[:, i % NB, :, bass.ds((i // NB) * HD, HD)], oT[:, :, 0:HD],
                                        rden[:, :, :].to_broadcast([P, BLK // 32, HD]),
                                        ALU.mult).then_inc(attn_steps, 1)
                ve.wait_ge(attn_steps, 2 * i + 2)

            with ve.Fori(0, W_FREE) as i:
                drain_attention(i)
            ve.wait_ge(ffn_loaded, 16)
            QUARTER = FFN_COLS // 4
            for k in range(4):
                cols = slice(QUARTER * k, QUARTER * (k + 1))
                steps.then_wait(nc.vector.tensor_copy(w_hi[:, cols], w_raw[:, cols]))
                nc.vector.tensor_tensor(w_lo[:, cols], w_raw[:, cols], w_hi[:, cols].bitcast(fp32),
                                        ALU.subtract).then_inc(w_split, 1)
            ve.wait_ge(w_split, 4)
            drain_attention(W_FREE)
            for k in range(4):
                part = w_lo[:, QUARTER * k:QUARTER * (k + 1)].bitcast(fp32)
                nc.vector.tensor_reduce(low_range[:, 0, k:k + 1], part, AX.X, ALU.max)
                last = nc.vector.tensor_reduce(low_range[:, 1, k:k + 1], part, AX.X, ALU.min, negate=True)
            steps.then_wait(last)
            steps.then_wait(nc.vector.reduce_max(low_nonzero[:, :], low_range[:, :, :].rearrange("p s k -> p (s k)"),
                                                 AX.X))
            nc.vector.tensor_scalar(low_nonzero[:, :], low_nonzero[:, :], 0.0, None, ALU.is_gt).then_inc(low_any, 1)
            drain_attention(W_FREE + 1)
            ve.wait_ge(inexact_psum, 1)
            nc.vector.tensor_scalar(inexact[:, :], PS[0:1, MISC, 0:1], INEXACT, None, ALU.is_gt
                                    ).then_inc(inexact_ready, 1)

            def statistics(n, src):
                for t in range(TPB):
                    last = nc.vector.bn_stats(stats[:, 0, t, :], src[:, t, :])
                steps.then_wait(last)
                for t in range(TPB):
                    last = nc.vector.bn_aggr(mv[:, n % NB, t, :], stats[:, 0, t, :])
                last.then_inc(tail_var, 1)

            def apply_norm(n, dst, src):
                ve.wait_ge(tail_rstd, n + 1)
                for t in range(TPB):
                    last = nc.vector.tensor_scalar(dst[:, t, :], src[:, t, :], mv[:, n % NB, t, 0:1],
                                                   rstd[:, n % NB, t:t + 1], ALU.subtract, ALU.mult)
                return last

            def untranspose(b):
                if b:
                    ve.wait_ge(proj_psum, b)
                nc.vector.transpose(oTn[:, :], attn[:, b, :, :].rearrange("p t d -> p (t d)")).then_inc(oTn_ready, 1)

            def attn_out(b):
                ve.wait_ge(proj_psum, b + 1)
                ve.wait_ge(rest_loaded, 16)
                for t in range(TPB):
                    last = nc.vector.tensor_tensor(ao[:, t, :], PS[:, MISC, D * t:D * (t + 1)],
                                                   rest[:, X_BO:X_BO + D], ALU.add)
                last.then_inc(proj_drained, 1)
                ve.wait_ge(proj_drained, b + 1)
                statistics(2 * b, ao)

            def residual(b):
                steps.then_wait(apply_norm(2 * b, ln, ao))
                ve.wait_ge(x_again[b % 2], 16 * (b // 2 + 1))
                nc.vector.tensor_tensor(x1(b), xr[:, b % 2, :, :], ln[:, :, :], ALU.add).then_inc(x1_ready, 1)
                ve.wait_ge(x1_ready, b + 1)
                statistics(2 * b + 1, x1(b))

            def second_norm(b):
                apply_norm(2 * b + 1, ln2, x1(b)).then_inc(ln2_ready, 1)

            def drain_xT(b):
                ve.wait_ge(xT_psum, b + 1)
                steps.then_wait(nc.vector.tensor_copy(xT_hi[:, tokens(b)], PS[:, MISC, :]))
                nc.vector.tensor_tensor(xT_lo[:, tokens(b)], PS[:, MISC, :], xT_hi[:, tokens(b)].bitcast(fp32),
                                        ALU.subtract).then_inc(xT_ready, 1)
                ve.wait_ge(xT_ready, b + 1)

            def gate(n):
                c, slot = n % FC, n % 2
                ve.wait_ge(gate_psum, 2 * n + 2)
                ve.wait_ge(silu_ready, n + 1)
                if n >= 2:
                    ve.wait_ge(g_low, n - 1)
                nc.vector.scalar_tensor_tensor(act_f[:, slot, :], PS[:, 2 + slot, :],
                                               rest[:, X_S + FC + c:X_S + FC + c + 1], silu[:, slot, :],
                                               ALU.mult, ALU.mult).then_inc(gated_ready, 1)

            chain = (untranspose, attn_out, residual, second_norm, drain_xT)
            for b in range(NB - 1):
                for stage in chain:
                    stage(b)
                drain_attention(EARLY + b)
            b = NB - 1
            untranspose(b)
            between = {1: attn_out, 3: residual, 5: second_norm, 7: drain_xT}
            for n in range(FC * NB):
                gate(n)
                if n in between:
                    between[n](b)
            n = 0
            for stage in STAGES:
                b = int(stage[1])
                if stage[0] in "BC":
                    hi, lo = hidden_dst(stage)
                    for c in range(FC):
                        ve.wait_ge(h_high, FC * NB + n + 1)
                        nc.vector.tensor_tensor(lo[:, c, :], act_f[:, n % 2, :], hi[:, c, :].bitcast(fp32),
                                                ALU.subtract).then_inc(h_low, 1)
                        n += 1
                elif stage[0] == "Z":
                    ve.wait_ge(y_tokens, b + 1)
                    y = PS[:, 2 + b % 2, :].rearrange("p (t d) -> p t d", d=D)
                    statistics(2 * NB + b, y)
                    apply_norm(2 * NB + b, ln, y).then_inc(y_drained, 1)
                    ve.wait_ge(y_drained, b + 1)
                    nc.vector.tensor_tensor(x1(b), x1(b), ln[:, :, :], ALU.add).then_inc(y_ready, 1)
                    ve.wait_ge(y_ready, b + 1)

        @block.tensor
        def _(pe):
            mm = nc.tensor.matmul

            def weight(col):
                return wp[:, col:col + D]

            def keep_warm(n):
                for _ in range(n):
                    mm(PS[:, 5, :], warm[:, 0:P], warm[:, :], start=True, stop=True)

            def transpose_tiles(bank, src):
                for t in range(TPB):
                    last = nc.tensor.transpose(PS[:, bank, D * t:D * (t + 1)], src[:, t, :], ident[:, :])
                return last

            def transpose_x(b):
                pe.wait_ge(xn_ready, b + 1)
                if b >= 2:
                    pe.wait_ge(v_drained, b - 1)
                elif b:
                    pe.wait_ge(xnT_ready, b)
                transpose_tiles(MISC, xs[:, tiles(b), :]).then_inc(xnT_psum, 1)

            def down(b):
                pe.wait_ge(xnT_ready, b + 1)
                if b:
                    pe.wait_ge(ct_ready, b)
                mm(PS[:, ACC, :], weight(W_D), xnT[:, tokens(b)], start=True, stop=True).then_inc(ct_psum, 1)

            def project_side(m):
                b = m % NB
                content, rotated, swapped = side_banks(m)
                src, cols = (xnT, (W_KC, W_KR, W_KS)) if m < NB else (ct, (W_QC, W_QR, W_QS))
                if m < NB:
                    pe.wait_ge(ct_ready, b + 1)
                if m >= 2:
                    pe.wait_ge(side_drained, m - 1)
                mm(PS[:, rotated, :], weight(cols[1]), src[:, tokens(b)], start=True, stop=True)
                mm(PS[:, swapped, :], weight(cols[2]), src[:, tokens(b)], start=True, stop=True)
                mm(PS[:, content, :], weight(cols[0]), ct[:, tokens(b)], start=True, stop=True).then_inc(side_psum, 1)

            def project_v(b):
                pe.wait_ge(xnT_ready, min(b + 2, NB))
                if b == NB - 1:
                    pe.wait_ge(v_drained, b)
                for t in range(TPB):
                    at = b * BLK + t * P
                    last = mm(PS[:, MISC, D * t:D * (t + 1)], ct[:, at:at + P], weight(W_V), start=True, stop=True)
                last.then_inc(v_psum, 1)

            def norm(m):
                pe.wait_ge(squares_ready, m + 1)
                if m >= 2:
                    pe.wait_ge(norm_reduced, m - 1)
                mm(PS[0:H, norm_bank(m), :], sel_bf, squares[:, m // NB, tokens(m % NB)],
                   start=True, stop=True).then_inc(norm_psum, 1)

            pe.wait_ge(pool_constants, 1)
            keep_warm(WARM_START)
            pe.wait_ge(ident_loaded, 16)
            transpose_x(0)
            pe.wait_ge(weights_loaded, 16)
            down(0)
            transpose_x(1)
            down(1)
            project_side(0)
            project_v(0)
            for b in range(1, NB):
                project_side(b)
                if b + 1 < NB:
                    transpose_x(b + 1)
                    down(b + 1)
                project_v(b)
            pe.wait_ge(dve_constants, 2)
            pe.wait_ge(v_drained, NB)
            for b in range(NB):
                project_side(NB + b)
                for m in NORMS_AFTER[b]:
                    norm(m)

            keep_warm(WARM_FLAG)
            pe.wait_ge(product_ready, 1)
            mm(PS[0:1, 0, 0:H], norm_prod[:, :], ident[0:H, 0:H], start=True, stop=True).then_inc(product_psum, 1)

            keep_warm(WARM_FLAG)
            pe.wait_ge(flag_ready, 1)
            general = pe.value_load(unsafe[0:1, 0:1], min_val=0, max_val=1)
            with pe.If(general > 0):
                nq = GH * TPB
                pe.wait_ge(operands_in, operands_of(NI - 1))
                with pe.Fori(0, NI) as i:
                    for u in range(2 * nq):
                        j, t, h = u // (2 * TPB), u // 2 % TPB, u % 2
                        if u >= 2:
                            pe.wait_ge(max_reduced, 2 * nq * i + (u - 1))
                        for k in range(2):
                            last = mm(PS[:, 2 * h + k, :], QT[:, i, j, P * t:P * (t + 1)],
                                      KT[:, i // NB, j, (2 * h + k) * BLK:(2 * h + k + 1) * BLK],
                                      start=True, stop=True)
                        last.then_inc(max_scores, 1)
                    pe.wait_ge(max_steps, 5 * i + 5)
                    pe.wait_ge(shift_rows_ready, i + 1)
                    nc.tensor.transpose(PS[:, MISC, 0:P // 2].bitcast(bf16), shift_cols[:, :],
                                        ident_bf[:, :]).then_inc(shift_psum, 1)
                pe.wait_ge(shift_in, 16 * SPLIT * NI)

            def fill(i, t, half):
                dst = unit(pe, (2 * NT * i + (2 * t + half)) % UNITS)
                for k in range(2):
                    j = 2 * half + k
                    last = mm(dst[:, BLK * k:BLK * (k + 1)], KT[:, i // NB, j, P * t:P * (t + 1)], QT[:, i, j, :],
                              start=True, stop=True)
                last.then_inc(scores_ready, 1)

            def attend(i, inserts):
                filling_next = not (isinstance(i, int) and i == NI - 1)
                for t in range(NT):
                    ahead = t + 2
                    fi, ft = (i, ahead) if ahead < NT else (i + 1, ahead - NT)
                    filling = ahead < NT or filling_next
                    if filling:
                        if ahead == NT:
                            pe.wait_ge(operands_in, operands_of(fi))
                        pe.wait_ge(probs_ready, 2 * NT * i + (2 * ahead - 2))
                        fill(fi, ft, 0)
                    pe.wait_ge(probs_ready, 2 * NT * i + (2 * t + 2))
                    if t == 0:
                        pe.wait_ge(acc_free, i + 1)
                        pe.wait_ge(v_staged, 2 * (i // NB) + 1)
                    if t == NT // 2:
                        pe.wait_ge(v_staged, 2 * (i // NB) + 2)
                    for j in range(GH):
                        last = mm(PS[32 * j:32 * j + VW, ACC, :], Vst[:, t, VW * j:VW * (j + 1)], probs[:, t % 4, j, :],
                                  start=t == 0, stop=t == NT - 1)
                    last.then_inc(probs_used, 1)
                    if filling:
                        pe.wait_ge(probs_ready, 2 * NT * i + (2 * ahead - 1))
                        fill(fi, ft, 1)
                    if t in inserts:
                        inserts[t]()

            def project(b):
                pe.wait_ge(oTn_ready, b + 1)
                pe.wait_ge(rest_loaded, 16)
                if b:
                    pe.wait_ge(xT_ready, b)
                else:
                    pe.wait_ge(inexact_ready, 1)
                for t in range(TPB):
                    last = mm(PS[:, MISC, D * t:D * (t + 1)], oTn[:, P * t:P * (t + 1)], rest[:, X_WO:X_WO + D],
                              start=True, stop=True)
                last.then_inc(proj_psum, 1)

            def count_inexact():
                pe.wait_ge(low_any, 1)
                mm(PS[0:1, MISC, 0:1], low_nonzero[:, :], ones[:, :], start=True, stop=True).then_inc(inexact_psum, 1)

            def transpose_x2(b):
                pe.wait_ge(ln2_ready, b + 1)
                transpose_tiles(MISC, ln2).then_inc(xT_psum, 1)

            pe.wait_ge(acc_free, 1)
            pe.wait_ge(operands_in, operands_of(0))
            fill(0, 0, 0)
            fill(0, 0, 1)
            fill(0, 1, 0)
            pe.wait_ge(probs_ready, 1)
            fill(0, 1, 1)
            with pe.Fori(0, EARLY) as i:
                attend(i, {})
            attend(EARLY, {2: count_inexact, 6: lambda: project(0), 13: lambda: transpose_x2(0)})
            attend(EARLY + 1, {6: lambda: project(1), 13: lambda: transpose_x2(1)})
            attend(EARLY + 2, {6: lambda: project(2), 13: lambda: transpose_x2(2)})

            def feed_forward(with_low):
                def product(out_ap, at, rhs_hi, rhs_lo, start, stop):
                    hi, lo = w_hi[:, at:at + P], w_lo[:, at:at + P]
                    mm(out_ap, hi, rhs_hi, start=start, stop=False)
                    last = mm(out_ap, hi, rhs_lo, start=False, stop=stop and not with_low)
                    if with_low:
                        last = mm(out_ap, lo, rhs_hi, start=False, stop=stop)
                    return last

                def gates(n):
                    b, c, slot = n // FC, n % FC, n % 2
                    if c == 0:
                        pe.wait_ge(xT_ready, b + 1)
                    if n >= 2:
                        pe.wait_ge(silu_ready, n - 1)
                    product(PS[:, slot, :], X_W1 + P * c, xT_hi[:, tokens(b)], xT_lo[:, tokens(b)],
                            True, True).then_inc(gate_psum, 1)
                    if n >= 2:
                        pe.wait_ge(gated_ready, n - 1)
                    product(PS[:, 2 + slot, :], X_W2 + P * c, xT_hi[:, tokens(b)], xT_lo[:, tokens(b)],
                            True, True).then_inc(gate_psum, 1)

                pe.wait_ge(w_split, 4)
                b = NB - 1
                for n in range(FC * NB):
                    gates(n)
                    if n == 1:
                        project(b)
                    if n == 7:
                        transpose_x2(b)

                n = 0
                for stage in STAGES:
                    b = int(stage[1])
                    if stage[0] in "BC":
                        hi, lo = hidden_src(stage)
                        w = X_H1 if stage[0] == "B" else X_H2
                        pe.wait_ge(*parts_of(stage))
                        for c in range(FC):
                            if n >= 2:
                                pe.wait_ge(gelu_ready, n - 1)
                            for k in range(FC):
                                last = product(PS[:, 4 + n % 2, :], w + F * k + P * c, hi[:, k, :], lo[:, k, :],
                                               k == 0, k == FC - 1)
                            last.then_inc(hidden_psum, 1)
                            n += 1
                    elif stage[0] == "Y":
                        hi, lo = hidden_src(stage)
                        pe.wait_ge(*parts_of(stage))
                        if b >= 2:
                            pe.wait_ge(yT_ready, b - 1)
                        for k in range(FC):
                            last = product(PS[:, b % 2, :], X_W3 + D * k, hi[:, k, :], lo[:, k, :], k == 0, k == FC - 1)
                        last.then_inc(y_psum, 1)
                    else:
                        pe.wait_ge(yT_ready, b + 1)
                        if b >= 2:
                            pe.wait_ge(y_drained, b - 1)
                        transpose_tiles(2 + b % 2, yT[:, b % 2, :].rearrange("p (t n) -> p t n", n=P)
                                        ).then_inc(y_tokens, 1)

            some_low = pe.value_load(inexact[0:1, 0:1], min_val=0, max_val=1)
            with pe.If(some_low > 0):
                feed_forward(True)
            with pe.If(some_low < 1):
                feed_forward(False)


def setup_pack(i):
    a = {k[len("L0_attn_"):]: np.asarray(v) for k, v in i.items() if k.startswith("L0_attn_")}
    R = D // 2
    pack = np.zeros((P, SETUP_COLS), np.float32)

    def swapped(w):
        return w.reshape(w.shape[:-1] + (D // 2, 2))[..., ::-1].reshape(w.shape)

    pack[:, W_D:W_D + R], pack[:, W_D + R:W_D + D] = a["Wd_q_w"], a["Wd_kv_w"]
    pack[:R, W_QC:W_QC + D] = a["Wu_q_w"]
    pack[:R, W_QR:W_QR + D] = a["Wq_r_w"]
    pack[:R, W_QS:W_QS + D] = swapped(a["Wq_r_w"])
    pack[R:, W_KC:W_KC + D] = a["Wu_k_w"]
    pack[:, W_KR:W_KR + D] = a["Wk_r_w"]
    pack[:, W_KS:W_KS + D] = swapped(a["Wk_r_w"])
    pack[R:, W_V:W_V + D] = a["Wu_v_w"]
    pack[:, B_V:B_V + D] = a["Wu_v_b"]
    for h in range(H):
        pack[HD * h:HD * (h + 1), SEL + h] = 1
    pack[:R, BIAS], pack[R:, BIAS] = a["Wd_q_b"], a["Wd_kv_b"]
    for n, b in enumerate((a["Wu_q_b"], a["Wq_r_b"], swapped(a["Wq_r_b"]),
                           a["Wu_k_b"], a["Wk_r_b"], swapped(a["Wk_r_b"]))):
        pack[:, BIAS + 1 + n] = b
    return pack


def ffn_pack(i):
    f = {k[len("L0_ffn_"):]: np.asarray(v) for k, v in i.items() if k.startswith("L0_ffn_")}
    pack = np.zeros((P, FFN_COLS), np.float32)
    pack[:, X_W1:X_W1 + F], pack[:, X_W2:X_W2 + F] = f["w1_w"].T, f["w2_w"].T
    for k in range(FC):
        pack[:, X_H1 + F * k:X_H1 + F * (k + 1)] = f["h1_w"].T[P * k:P * (k + 1)]
        pack[:, X_H2 + F * k:X_H2 + F * (k + 1)] = f["h2_w"].T[P * k:P * (k + 1)]
        pack[:, X_W3 + D * k:X_W3 + D * (k + 1)] = f["w3_w"].T[P * k:P * (k + 1)]
    return pack


def rest_pack(i):
    pack = np.zeros((P, REST_COLS), np.float32)
    wo = np.asarray(i["L0_attn_Wo_w"])
    for g in range(NG):
        for j in range(GH):
            r = HD * (GH * g + j)
            at = 32 * j + HD * g
            pack[at:at + HD, X_WO:X_WO + D] = wo[r:r + HD]
    pack[:, X_BO:X_BO + D] = np.asarray(i["L0_attn_Wo_b"])
    for n, name in enumerate(("w1_s", "w2_s", "h1_s", "h2_s")):
        pack[:, X_S + FC * n:X_S + FC * (n + 1)] = np.asarray(i["L0_ffn_" + name]).reshape(FC, P).T
    pack[:, X_S + 4 * FC] = np.asarray(i["L0_ffn_w3_s"])
    return pack


def rotation_tables():
    pos = np.arange(T, dtype=np.float32)
    ids = np.arange(D // 2, dtype=np.float32)
    theta = (np.float32(10000.0) ** (np.float32(-2.0) * ids)).astype(np.float32) / np.float32(D // 2)
    angle = theta[:, None] * pos[None, :]
    cos = np.repeat(np.cos(angle), 2, axis=0).astype(np.float32)
    sin = np.repeat(np.sin(angle), 2, axis=0).astype(np.float32)
    sin[0::2] = -sin[0::2]
    return cos, sin


def kernel(**inputs):
    import concourse.bacc as bacc
    from concourse.bass_utils import run_bass_kernel_spmd

    cos, sin = rotation_tables()
    arrays = {
        "x": np.ascontiguousarray(np.asarray(inputs["L0_attn_x"])[0]),
        "setup": setup_pack(inputs),
        "ffn": ffn_pack(inputs),
        "rest_of_tail": rest_pack(inputs),
        "cos": cos,
        "sin": sin,
        "identity": np.eye(P, dtype=np.float32),
    }
    nc = bacc.Bacc("TRN2", target_bir_lowering=False, num_devices=1)
    fp32 = mybir.dt.float32
    args = [nc.dram_tensor(name, a.shape, fp32, kind="ExternalInput").ap() for name, a in arrays.items()]
    for name in ("q_scratch", "k_scratch"):
        args.append(nc.dram_tensor(name, (D, SPLIT, T), mybir.dt.bfloat16, kind="Internal").ap())
    args.append(nc.dram_tensor("out", (T, D), fp32, kind="ExternalOutput").ap())
    layer(nc, *args)
    result = run_bass_kernel_spmd(nc, [arrays], core_ids=[0])
    return result.results[0]["out"].reshape(1, T, D)
```

```python
from contextlib import ExitStack

import concourse.bass as bass
from concourse import mybir
import numpy as np

T, D, H, HD, F = 2048, 128, 16, 8, 512
P = 128
BLK = 512
NB = T // BLK
NT = T // P
TPB = BLK // P
NG, GH = 4, 4
NI = NG * NB
VW = HD + 1
FC = F // P
SPLIT = 3
ROWS = SPLIT * SPLIT * HD
EPS = 1e-5
INEXACT = 0.5
SCORE_SCALE = 1.0 / 12.0
SAFE_SCORE = 60.0
SAFE_PRODUCT = 0.98 * (SAFE_SCORE / SCORE_SCALE) ** 2

ONE_PAIR = float(np.array([0x3F803F80], np.uint32).view(np.float32)[0])

(W_D, W_QC, W_QR, W_QS, W_KC, W_KR, W_KS, W_V, B_V) = (D * n for n in range(9))
SEL = 9 * D
BIAS = SEL + H
SETUP_COLS = BIAS + 7
X_W1, X_W2 = 0, F
X_H1, X_H2 = 2 * F, 2 * F + FC * F
X_W3 = 2 * F + 2 * FC * F
FFN_COLS = X_W3 + FC * D
X_WO = 0
X_BO = X_WO + D
X_S = X_BO + D
REST_COLS = X_S + 4 * FC + 1
WARM_START, WARM_NORM, WARM_FLAG = 13, 5, 5
EARLY = NI - NB + 1


class Steps:

    def __init__(self, engine, sem):
        self.engine, self.sem, self.n = engine, sem, 0

    def mark(self, instruction):
        instruction.then_inc(self.sem, 1)
        self.n += 1
        return self.n

    def then_wait(self, instruction):
        self.engine.wait_ge(self.sem, self.mark(instruction))


def layer(nc, x_dram, setup_dram, ffn_dram, rest_dram, cos_dram, sin_dram, ident_dram, q_scratch, k_scratch, out):
    fp32, fp32r, bf16, int32 = mybir.dt.float32, mybir.dt.float32r, mybir.dt.bfloat16, mybir.dt.int32
    ALU, ACT, AX = mybir.AluOpType, mybir.ActivationFunctionType, mybir.AxisListType
    ctx = ExitStack()
    with ctx:
        size = {fp32: 4, fp32r: 4, bf16: 2, int32: 4}
        top = [-(-nc.sbuf_base // 32) * 32]

        def over(name, shape, dt, at):
            return nc.alloc_sbuf_tensor_at(name, shape, dt, offset=at)

        def sb(name, shape, dt=fp32):
            at = top[0]
            top[0] += -(-int(np.prod(shape[1:])) * size[dt] // 32) * 32
            return over(name, shape, dt, at)

        def sem(name):
            return ctx.enter_context(nc.semaphore(name))

        SLOTS = 4
        QUARTERS = 4
        at_QT = top[0]
        QT = sb("q_operand", [P, NI, GH, BLK], bf16)
        at_KT = top[0]
        KT = sb("k_operand", [P, NG, GH, T], bf16)
        at_probs = top[0]
        probs = sb("probs", [P, SLOTS, GH, BLK])
        at_split = top[0]
        Ks = sb("k_split", [P, SPLIT, T], bf16)
        Qs = sb("q_split", [P, SPLIT, T], bf16)
        at_V = top[0]
        V = sb("v_all", [P, NT, NG, GH * VW])
        Vst = sb("v_group", [P, NT, GH * VW])
        attn = sb("attn", [P, NB, BLK // 32, NG * HD])
        ident = sb("ident", [P, P])
        ident_bf = sb("ident_bf", [P, P], bf16)
        oT = sb("o_tokens", [P, BLK // 32, 32])
        rden = sb("rden", [P, BLK // 32, 1])
        stats = sb("stats", [P, NB, TPB, 6])
        mv = sb("mean_var", [P, NB, TPB, 2])
        rstd = sb("rstd", [P, NB, TPB])
        minus_half = sb("minus_half", [P, TPB])
        norm_max = sb("norm_max", [P, 2])
        side_max = sb("side_max", [1, 2])
        unsafe = sb("unsafe", [1, 1], int32)
        half_max = sb("half_max", [P, GH * TPB, 2])
        neg_max = sb("neg_max", [P, GH * TPB])
        neg_rest = sb("neg_rest", [P, GH * TPB])
        shift_cols = sb("shift_cols", [P, P], bf16)
        shift_rows = sb("shift_rows", [P, P], bf16)
        ones = sb("ones", [P, 1])
        touch = sb("touch", [1, 1])
        low_range = sb("low_range", [P, 2, QUARTERS])
        low_nonzero = sb("low_nonzero", [P, 1])
        inexact = sb("inexact", [1, 1], int32)
        assert top[0] <= nc.sbuf_usable_end
        shift_parts = shift_cols[:, 0:SPLIT * GH * TPB].rearrange("p (s q) -> p s q", s=SPLIT)

        PS = ctx.enter_context(nc.psum_tensor("psum", [P, 8, BLK], fp32))
        UNITS = 3
        ACC, MISC = 6, 7

        probs_f = probs[:, :, :, :].rearrange("p a b c -> p (a b c)")
        xs = probs_f[:, 0:T].rearrange("p (t d) -> p t d", d=D)
        xnT = probs_f[:, T:2 * T]
        ct = probs_f[:, 2 * T:3 * T]
        squares = probs_f[:, 3 * T:4 * T].bitcast(bf16).rearrange("p (s t) -> p s t", s=2)
        KT_f = KT[:, :, :, :].rearrange("p g j n -> p (g j n)").bitcast(fp32)
        QT_f = QT[:, :, :, :].rearrange("p i j n -> p (i j n)").bitcast(fp32)
        GF = GH * T // 2
        cosT, sinT = KT_f[:, 3 * GF:3 * GF + T], KT_f[:, 3 * GF + T:4 * GF]
        wp = KT_f[:, 2 * GF:2 * GF + SETUP_COLS]
        tmp = QT_f[:, 3 * GF:4 * GF].rearrange("p (s k n) -> p s k n", s=2, n=BLK)
        sel_bf = QT_f[:, 2 * GF:2 * GF + H // 2].bitcast(bf16)
        warm = oT[:, :, :].rearrange("p b d -> p (b d)")[:, 0:BLK // 2].bitcast(bf16)

        PER_I, PER_G = GH * BLK * 2, GH * T * 2
        w_raw = over("w_raw", [P, FFN_COLS], fp32, at_split)
        w_hi = over("w_hi", [P, FFN_COLS], fp32r, at_QT)
        w_lo = over("w_lo", [P, FFN_COLS], fp32r, at_QT + 4 * FFN_COLS)
        W_FREE = -(-8 * FFN_COLS // PER_I)
        rest_t = over("rest", [P, REST_COLS], fp32, at_QT + PER_I * W_FREE)
        rest = rest_t[:, :]
        xr = over("x_residual", [P, 2, TPB, D], fp32, at_QT + PER_I * (W_FREE + 1))
        yT = over("y_T", [P, 2, BLK], fp32, at_QT + PER_I * (W_FREE + 2))
        assert W_FREE == 11 and 4 * REST_COLS <= PER_I
        h_hi = [over(f"h_hi{b}", [P, FC, BLK], fp32r, at_KT + PER_G * b) for b in range(NB)]
        h_lo = [over(f"h_lo{b}", [P, FC, BLK], fp32r, at_KT + PER_G * b + PER_G // 2) for b in range(NB)]
        h2_hi = [over(f"h2_hi{s}", [P, FC, BLK], fp32r, at_probs + PER_G * s) for s in range(2)]
        h2_lo = [over(f"h2_lo{s}", [P, FC, BLK], fp32r, at_probs + PER_G * s + PER_G // 2) for s in range(2)]
        oTn = over("attn_T", [P, BLK], fp32, at_V)
        xT_hi = over("xT_hi", [P, T], fp32r, at_split)
        xT_lo = over("xT_lo", [P, T], fp32r, at_split + 4 * T)
        ao = over("attn_out", [P, TPB, D], fp32, at_split + 8 * T)
        ln = over("ln", [P, TPB, D], fp32, at_split + 8 * T + 4 * BLK)
        ln2 = over("ln2", [P, TPB, D], fp32, at_split + 8 * T + 8 * BLK)
        h_raw = [over(f"h_raw{b}", [P, FC, BLK], fp32, at_KT + PER_G * b + PER_G // 2) for b in range(NB)]
        h2_raw = [over(f"h2_raw{s}", [P, FC, BLK], fp32, at_probs + PER_G * s + PER_G // 2) for s in range(2)]
        SILUS = 4
        silu = over("silu", [P, SILUS, BLK], fp32, at_QT + PER_I * (W_FREE + 3))

        def x1(b):
            return attn[:, b, :, :].rearrange("p t d -> p (t d)").rearrange("p (t d) -> p t d", d=D)

        x_loaded = [sem(f"x_loaded{b}") for b in range(NB)]
        tables_loaded = [sem(f"tables_loaded{b}") for b in range(NB)]
        weights_loaded, ident_loaded = sem("weights_loaded"), sem("ident_loaded")
        ffn_loaded, rest_loaded = sem("ffn_loaded"), sem("rest_loaded")
        x_again = [sem(f"x_again{s}") for s in range(2)]
        stored = sem("stored")
        operands_in = sem("operands_in")
        pool = sem("pool_steps")
        dve = sem("dve_steps")
        pool_constants, act_constants = sem("pool_constants"), sem("act_constants")
        xn_ready = sem("xn_ready")
        var_ready, rstd_ready = sem("var_ready"), sem("rstd_ready")
        xnT_psum, xnT_ready, ct_psum, ct_ready = sem("xnT_psum"), sem("xnT_ready"), sem("ct_psum"), sem("ct_ready")
        side_psum, side_drained, side_ready = sem("side_psum"), sem("side_drained"), sem("side_ready")
        v_psum, v_drained = sem("v_psum"), sem("v_drained")
        high_ready, squares_ready = sem("high_ready"), sem("squares_ready")
        rest_ready, mid_ready, low_ready = sem("rest_ready"), sem("mid_ready"), sem("low_ready")
        norm_psum, norm_reduced = sem("norm_psum"), sem("norm_reduced")
        side_max_psum, flag_ready = sem("side_max_psum"), sem("flag_ready")
        k_pads, q_pads = sem("k_pads"), sem("q_pads")
        max_scores, max_reduced, max_steps = sem("max_scores"), sem("max_reduced"), sem("max_steps")
        shift_psum, shift_rows_ready, shift_in = sem("shift_psum"), sem("shift_rows_ready"), sem("shift_in")
        scores_ready, probs_ready, probs_used = sem("scores_ready"), sem("probs_ready"), sem("probs_used")
        v_staged, acc_free, attn_steps = sem("v_staged"), sem("acc_free"), sem("attn_steps")
        w_split, touched = sem("w_split"), sem("touched")
        low_any, inexact_psum, inexact_ready = sem("low_any"), sem("inexact_psum"), sem("inexact_ready")
        oTn_ready = sem("oTn_ready")
        proj_psum, proj_drained, x1_ready, ln2_ready = (
            sem("proj_psum"), sem("proj_drained"), sem("x1_ready"), sem("ln2_ready"))
        xT_psum, xT_ready = sem("xT_psum"), sem("xT_ready")
        gate_psum, silu_ready, gated_ready = sem("gate_psum"), sem("silu_ready"), sem("gated_ready")
        hidden_psum, gelu_ready = sem("hidden_psum"), sem("gelu_ready")
        h_high = sem("h_high")
        g_low, h_low = sem("g_low"), sem("h_low")
        y_psum, yT_ready, y_tokens, y_drained, y_ready = (
            sem("y_psum"), sem("yT_ready"), sem("y_tokens"), sem("y_drained"), sem("y_ready"))
        out_done = sem("out_done")

        def tokens(b):
            return slice(b * BLK, (b + 1) * BLK)

        def tiles(b):
            return slice(b * TPB, (b + 1) * TPB)

        K_DMAS, Q_DMAS = SPLIT, 1

        def operands_of(i):
            return 16 * (K_DMAS + NB * Q_DMAS) * (i // NB) + 16 * Q_DMAS * (i % NB) + 16 * (K_DMAS + Q_DMAS)

        ORDER = ("G0 G1 G2 B0 B1 G3 C0 B2 C1 Y0 B3.0 B3.1 Z0 B3.2 A0 B3.3 Y1 C2.0 C2.1 Z1 C2.2 A1 C2.3 "
                 "C3.0 Y2 C3.1 Z2 C3.2 C3.3 A2 Y3 Z3 A3").split()
        STEPS = [(s[0], int(s[1]), c) for s in ORDER
                 for c in ([int(s[3])] if "." in s else range(FC) if s[0] in "GBC" else [0])]
        PE_STEPS = [s for s in STEPS if s != ("C", 0, 0)]
        PE_STEPS.insert(PE_STEPS.index(("G", 3, 2)), ("C", 0, 0))
        HIDDEN = [s for s in STEPS if s[0] in "BC"]
        SPLITS = [s for s in STEPS if s[0] in "GBC"]

        def hidden_src(kind, b):
            return (h2_hi[b % 2], h2_lo[b % 2]) if kind == "C" else (h_hi[b], h_lo[b])

        def hidden_dst(kind, b):
            return (h_hi[b], h_raw[b], h_lo[b]) if kind == "C" else (h2_hi[b % 2], h2_raw[b % 2], h2_lo[b % 2])

        def split_done(kind, b, k):
            if kind == "B":
                return g_low, FC * b + k + 1
            return h_low, HIDDEN.index(({"C": "B", "Y": "C"}[kind], b, k)) + 1

        K_SIDE, Q_SIDE = 0, 1
        SIDES = [(Q_SIDE, 0)] + [(K_SIDE, b) for b in range(NB)] + [(Q_SIDE, b) for b in range(1, NB)]

        def split_of(m):
            kind, b = SIDES[m]
            return (Ks if kind == K_SIDE else Qs)[:, :, tokens(b)]

        def hidden_bank(n):
            return 4 + n % 3

        def side_banks(m):
            return (0, 1, 2) if m % 2 == 0 else (3, 4, 5)

        def v_bank(b):
            return (MISC, ACC, ACC, 1)[b]

        scores = PS[:, 0:2 * UNITS, :].rearrange("p b n -> p (b n)")

        def unit(u):
            return scores[:, 2 * BLK * u:2 * BLK * (u + 1)] if isinstance(u, int) else \
                scores[:, bass.ds(u * (2 * BLK), 2 * BLK)]

        block = ctx.enter_context(nc.Block())

        @block.sync
        def _(sp):
            for b in range(NB):
                sp.dma_start(xs[:, tiles(b), :],
                             x_dram[tokens(b), :].rearrange("(t p) d -> p t d", p=P)).then_inc(x_loaded[b], 16)
            for b in range(NB):
                sp.dma_start(cosT[:, tokens(b)], cos_dram[:, tokens(b)]).then_inc(tables_loaded[b], 16)
                sp.dma_start(sinT[:, tokens(b)], sin_dram[:, tokens(b)]).then_inc(tables_loaded[b], 16)

            k_rows = k_scratch.rearrange("a (g d j) n -> g a d (j n)", g=NG, d=HD)
            q_rows = q_scratch.rearrange("t b a (g d j) n -> t g (b a) d (j n)", g=NG, d=HD)

            def lay_out_k(g):
                for b in range(SPLIT):
                    r = SPLIT * HD * b
                    sp.dma_start(KT[r:r + SPLIT * HD, g, :, :].rearrange("p j n -> p (j n)"), k_rows[g]
                                 ).then_inc(operands_in, 16)

            def lay_out_q(g, blk):
                sp.dma_start(QT[0:ROWS, NB * g + blk, :, :].rearrange("p j n -> p (j n)"), q_rows[blk, g]
                             ).then_inc(operands_in, 16)

            sp.wait_ge(k_pads, 1)
            sp.wait_ge(q_pads, 1)
            stores = 0
            for m, (kind, b) in enumerate(SIDES):
                sp.wait_ge(low_ready, m + 1)
                if kind == K_SIDE:
                    sp.dma_start(k_scratch[:, :, tokens(b)].rearrange("a p n -> p a n"), split_of(m)
                                 ).then_inc(stored, 16)
                    stores += 1
                    if b == NB - 1:
                        sp.wait_ge(stored, 16 * stores)
                        lay_out_k(0)
                else:
                    for a in range(SPLIT):
                        sp.dma_start(q_scratch[b, :, a, :, :].rearrange("b p n -> p b n"), split_of(m)
                                     ).then_inc(stored, 16)
                    stores += SPLIT
                    sp.wait_ge(stored, 16 * stores)
                    if b:
                        sp.wait_ge(operands_in, operands_of(b - 1))
                    lay_out_q(0, b)
            for g in range(1, NG):
                sp.wait_ge(k_pads, g + 1)
                sp.wait_ge(q_pads, g + 1)
                for b in range(NB):
                    sp.wait_ge(operands_in, operands_of(NB * g + b - 1))
                    if b == 0:
                        lay_out_k(g)
                    lay_out_q(g, b)

            sp.wait_ge(flag_ready, 1)
            general = sp.value_load(unsafe[0:1, 0:1], min_val=0, max_val=1)
            with sp.If(general > 0):
                with sp.Fori(0, NI) as i:
                    sp.wait_ge(shift_rows_ready, i + 2)
                    for s in range(SPLIT):
                        n = GH * TPB
                        sp.dma_start(QT[ROWS + s:ROWS + s + 1, i, :, :].rearrange("p j n -> p (j n)"),
                                     shift_rows[n * s:n * s + n, :]).then_inc(shift_in, 16)

            sp.wait_ge(operands_in, operands_of(NI - 1))
            sp.dma_start(w_raw[:, :], ffn_dram[:, :]).then_inc(ffn_loaded, 16)
            sp.wait_ge(probs_used, NT * (W_FREE + 1))
            sp.dma_start(rest, rest_dram[:, :]).then_inc(rest_loaded, 16)
            sp.wait_ge(probs_used, NT * (W_FREE + 2))
            for b in range(NB):
                if b >= 2:
                    sp.wait_ge(x1_ready, b - 1)
                sp.dma_start(xr[:, b % 2, :, :], x_dram[tokens(b), :].rearrange("(t p) d -> p t d", p=P)
                             ).then_inc(x_again[b % 2], 16)
            for b in range(NB):
                sp.wait_ge(y_ready, b + 1)
                sp.dma_start(out[tokens(b), :].rearrange("(t p) d -> p t d", p=P), x1(b)).then_inc(out_done, 16)
            sp.wait_ge(out_done, 16 * NB)

        @block.gpsimd
        def _(gp):
            steps = Steps(gp, pool)
            k_pad = KT_f[64:P, :].rearrange("p (g n) -> p g n", g=NG)
            q_pad = QT_f[64:P, :].rearrange("p (g n) -> p g n", g=NG)
            nc.gpsimd.memset(warm[:, :], 0.0).then_inc(pool_constants, 1)
            nc.gpsimd.memset(ones[:, :], 1.0)
            nc.gpsimd.memset(touch[:, :], 0.0)
            nc.gpsimd.memset(minus_half[:, :], -0.5).then_inc(pool_constants, 1)
            gp.wait_ge(pool_constants, 2)
            nc.gpsimd.memset(k_pad[:, 0, :], ONE_PAIR).then_inc(k_pads, 1)
            gp.wait_ge(k_pads, 1)

            def root(n):
                gp.wait_ge(var_ready, n + 1)
                out_rstd = rstd[:, n % NB, :]
                steps.then_wait(nc.gpsimd.tensor_scalar(out_rstd, mv[:, n % NB, :, 1], EPS, None, ALU.add))
                nc.gpsimd.tensor_tensor(out_rstd, out_rstd, minus_half[:, :], ALU.pow).then_inc(rstd_ready, 1)

            for n in range(NB):
                root(n)
            nc.gpsimd.memset(V[:, :, :, :].rearrange("p t g (j w) -> p (t g j) w", w=VW)[:, :, HD:VW],
                             1.0).then_inc(pool_constants, 1)
            gp.wait_ge(pool_constants, 3)
            nc.gpsimd.memset(q_pad[:, 0, :], 0.0).then_inc(q_pads, 1)
            gp.wait_ge(q_pads, 1)

            for m in range(2 * NB):
                part = split_of(m)
                gp.wait_ge(high_ready, m + 1)
                if m >= 2:
                    gp.wait_ge(low_ready, m - 1)
                nc.gpsimd.tensor_tensor(tmp[:, m % 2, 3, :], tmp[:, m % 2, 2, :], part[:, 0, :],
                                        ALU.subtract).then_inc(rest_ready, 1)
                gp.wait_ge(mid_ready, m + 1)
                nc.gpsimd.tensor_tensor(part[:, 2, :], tmp[:, m % 2, 3, :], part[:, 1, :],
                                        ALU.subtract).then_inc(low_ready, 1)

            def stage_v(g, half):
                t = slice(half * NT // 2, (half + 1) * NT // 2)
                nc.gpsimd.tensor_copy(Vst[:, t, :], V[:, t, g, :]).then_inc(v_staged, 1)

            gp.wait_ge(v_drained, NB // 2)
            stage_v(0, 0)
            gp.wait_ge(v_drained, NB)
            stage_v(0, 1)
            gp.wait_ge(v_staged, 2)
            gp.wait_ge(low_ready, 2 * NB)
            gp.wait_ge(squares_ready, 2 * NB)
            gp.wait_ge(side_ready, 2 * NB)
            gp.wait_ge(norm_psum, 2 * NB)
            for g in range(1, NG):
                nc.gpsimd.memset(k_pad[:, g, :], ONE_PAIR).then_inc(k_pads, 1)
                gp.wait_ge(k_pads, g + 1)
                nc.gpsimd.memset(q_pad[:, g, :], 0.0).then_inc(q_pads, 1)
                gp.wait_ge(q_pads, g + 1)
            with gp.Fori(1, NG) as g:
                gp.wait_ge(probs_used, NG * NT * g - NT // 2)
                stage_v(g, 0)
                gp.wait_ge(probs_used, NG * NT * g)
                stage_v(g, 1)


            for n in range(2 * (NB - 1)):
                root(NB + n)
            for n in range(FC * NB):
                if n == FC * (NB - 1):
                    root(3 * NB - 2)
                    root(3 * NB - 1)
                b, c = divmod(n, FC)
                gp.wait_ge(h_high, SPLITS.index(("G", b, c)) + 1)
                nc.gpsimd.tensor_tensor(h_lo[b][:, c, :], h_raw[b][:, c, :], h_hi[b][:, c, :].bitcast(fp32),
                                        ALU.subtract).then_inc(g_low, 1)
            for n in range(2 * NB, 3 * NB):
                root(NB + n)

        @block.scalar
        def _(act):
            act.dma_start(ident[:, :], ident_dram[:, :]).then_inc(ident_loaded, 16)
            act.dma_start(wp, setup_dram[:, :]).then_inc(weights_loaded, 16)
            act.wait_ge(ident_loaded, 16)
            nc.scalar.activation(ident_bf[:, :], ident[:, :], ACT.Copy).then_inc(act_constants, 1)
            act.wait_ge(weights_loaded, 16)
            nc.scalar.activation(sel_bf, wp[:, SEL:SEL + H], ACT.Copy).then_inc(act_constants, 1)

            def drain_xnT(b):
                act.wait_ge(xnT_psum, b + 1)
                nc.scalar.activation(xnT[:, tokens(b)], PS[:, MISC, :], ACT.Copy).then_inc(xnT_ready, 1)

            def drain_ct(b):
                act.wait_ge(ct_psum, b + 1)
                nc.scalar.activation(ct[:, tokens(b)], PS[:, ACC, :], ACT.Identity,
                                     bias=wp[:, BIAS:BIAS + 1]).then_inc(ct_ready, 1)

            def mid(m):
                act.wait_ge(rest_ready, m + 1)
                nc.scalar.activation(split_of(m)[:, 1, :], tmp[:, m % 2, 3, :], ACT.Copy).then_inc(mid_ready, 1)

            def high(m):
                nc.scalar.activation(split_of(m)[:, 0, :], tmp[:, m % 2, 2, :], ACT.Copy).then_inc(high_ready, 1)

            def square(m):
                kind, b = SIDES[m]
                nc.scalar.activation(squares[:, kind, tokens(b)], tmp[:, m % 2, 2, :],
                                     ACT.Square).then_inc(squares_ready, 1)

            drain_xnT(0)
            drain_ct(0)
            drain_xnT(1)
            for m in range(2 * NB):
                act.wait_ge(side_ready, m + 1)
                if m == 2 * NB - 1:
                    square(m)
                    high(m)
                else:
                    high(m)
                    square(m)
                if m + 1 < NB:
                    drain_ct(m + 1)
                if m + 2 < NB:
                    drain_xnT(m + 2)
                mid(m)

            act.wait_ge(norm_psum, 2 * NB)

            def exps(i, t, first=False):
                if not first:
                    act.wait_ge(probs_used, NT * i + (t - SLOTS + 1))
                for half in range(2):
                    act.wait_ge(scores_ready, 2 * NT * i + (2 * t + half + 1))
                    u = (2 * NT * i + (2 * t + half)) % UNITS
                    nc.scalar.activation(probs[:, t % SLOTS, 2 * half:2 * half + 2, :].rearrange("p j n -> p (j n)"),
                                         unit(u), ACT.Exp, scale=SCORE_SCALE).then_inc(probs_ready, 1)

            for t in range(SLOTS):
                exps(0, t, True)
            for t in range(SLOTS, NT):
                exps(0, t)
            with act.Fori(1, NI) as i:
                for t in range(NT):
                    exps(i, t)

            def preload(function):
                touches.then_wait(nc.scalar.activation(touch[:, :], touch[:, :], function))

            touches = Steps(act, touched)
            act.wait_ge(pool_constants, 2)
            preload(ACT.Silu)

            def gate_high(n):
                b, c = divmod(n, FC)
                act.wait_ge(gated_ready, n + 1)
                nc.scalar.activation(h_hi[b][:, c, :], h_raw[b][:, c, :], ACT.Copy).then_inc(h_high, 1)

            act.wait_ge(rest_loaded, 16)
            gated = None
            for kind, b, c in STEPS:
                if kind == "G":
                    n = FC * b + c
                    act.wait_ge(gate_psum, 2 * n + 1)
                    if n >= SILUS:
                        act.wait_ge(gated_ready, n - SILUS + 1)
                    nc.scalar.activation(silu[:, n % SILUS, :], PS[:, n % 2, :], ACT.Silu,
                                         scale=rest[:, X_S + c:X_S + c + 1]).then_inc(silu_ready, 1)
                if gated is not None:
                    gate_high(gated)
                    if kind != "G":
                        preload(ACT.Gelu)
                gated = n if kind == "G" else None
                if kind in "BC":
                    n = HIDDEN.index((kind, b, c))
                    hi, raw, _ = hidden_dst(kind, b)
                    col = X_S + (2 if kind == "B" else 3) * FC + c
                    act.wait_ge(hidden_psum, n + 1)
                    nc.scalar.activation(raw[:, c, :], PS[:, hidden_bank(n), :], ACT.Gelu,
                                         scale=rest[:, col:col + 1]).then_inc(gelu_ready, 1)
                    act.wait_ge(gelu_ready, n + 1)
                    nc.scalar.activation(hi[:, c, :], raw[:, c, :], ACT.Copy).then_inc(h_high, 1)
                    if (kind, b, c) == ("B", 1, 3):
                        preload(ACT.Silu)
                elif kind == "Y":
                    act.wait_ge(y_psum, b + 1)
                    if b >= 2:
                        act.wait_ge(y_tokens, b - 1)
                    nc.scalar.activation(yT[:, b % 2, :], PS[:, b % 2, :], ACT.Copy,
                                         scale=rest[:, X_S + 4 * FC:X_S + 4 * FC + 1]).then_inc(yT_ready, 1)

        @block.vector
        def _(ve):
            steps = Steps(ve, dve)
            def x_statistics(b):
                ve.wait_ge(x_loaded[b], 16)
                for t in range(TPB):
                    last = nc.vector.bn_stats(stats[:, b, t, :], xs[:, TPB * b + t, :])
                steps.then_wait(last)
                for t in range(TPB):
                    last = nc.vector.bn_aggr(mv[:, b, t, :], stats[:, b, t, :])
                last.then_inc(var_ready, 1)

            def normalise(b):
                ve.wait_ge(rstd_ready, b + 1)
                for t in range(TPB):
                    last = nc.vector.tensor_scalar(xs[:, TPB * b + t, :], xs[:, TPB * b + t, :], mv[:, b, t, 0:1],
                                                   rstd[:, b, t:t + 1], ALU.subtract, ALU.mult)
                last.then_inc(xn_ready, 1)

            def side(m):
                kind, b = SIDES[m]
                bias = BIAS + 4 if kind == K_SIDE else BIAS + 1
                content, rotated, swapped = side_banks(m)
                t1, t2, whole = (tmp[:, m % 2, k, :] for k in range(3))
                ve.wait_ge(side_psum, m + 1)
                ve.wait_ge(tables_loaded[b], 32)
                steps.mark(nc.vector.scalar_tensor_tensor(t1, PS[:, rotated, :], wp[:, bias + 1:bias + 2],
                                                          cosT[:, tokens(b)], ALU.add, ALU.mult))
                nc.vector.scalar_tensor_tensor(t2, PS[:, swapped, :], wp[:, bias + 2:bias + 3],
                                               sinT[:, tokens(b)], ALU.add, ALU.mult)
                ve.wait_ge(dve, steps.n)
                nc.vector.scalar_tensor_tensor(t1, PS[:, content, :], wp[:, bias:bias + 1], t1,
                                               ALU.add, ALU.add).then_inc(side_drained, 1)
                ve.wait_ge(side_drained, m + 1)
                if m >= 2:
                    ve.wait_ge(squares_ready, m - 1)
                    ve.wait_ge(rest_ready, m - 1)
                nc.vector.tensor_tensor(whole, t1, t2, ALU.add).then_inc(side_ready, 1)

            def values(b):
                ve.wait_ge(v_psum, b + 1)
                if b == 0:
                    ve.wait_ge(pool_constants, 3)
                for t in range(TPB):
                    last = nc.vector.tensor_tensor(
                        V[:, TPB * b + t, :, :].rearrange("p g (j w) -> p (g j) w", w=VW)[:, :, 0:HD],
                        PS[:, v_bank(b), D * t:D * (t + 1)].rearrange("p (h d) -> p h d", d=HD),
                        wp[:, B_V:B_V + D].rearrange("p (h d) -> p h d", d=HD), ALU.add)
                last.then_inc(v_drained, 1)

            x_statistics(0)
            for b in range(NB):
                if b + 1 < NB:
                    x_statistics(b + 1)
                normalise(b)
            ve.wait_ge(weights_loaded, 16)
            for m in range(NB + 1):
                side(m)
            values(0)
            values(1)
            side(NB + 1)
            side(NB + 2)
            side(NB + 3)
            values(2)

            ve.wait_ge(v_drained, NB - 1)
            nc.vector.memset(PS[:, ACC, :], 0.0).then_inc(acc_free, 1)
            ve.wait_ge(norm_psum, 2 * NB)
            nc.vector.reduce_max(norm_max[:, :], PS[:, MISC, :].rearrange("p (s n) -> p s n", s=2), AX.X
                                 ).then_inc(norm_reduced, 1)
            values(3)
            ve.wait_ge(side_max_psum, 1)
            steps.then_wait(nc.vector.reduce_max(side_max[:, :],
                                                 PS[0:1, 0, 0:2 * P].rearrange("p (s n) -> p s n", s=2), AX.X))
            nc.vector.tensor_scalar(unsafe[:, :], side_max[:, 0:1], side_max[:, 1:2], SAFE_PRODUCT,
                                    ALU.mult, ALU.is_gt).then_inc(flag_ready, 1)
            ve.wait_ge(flag_ready, 1)
            general = ve.value_load(unsafe[0:1, 0:1], min_val=0, max_val=1)
            with ve.If(general > 0):
                nq = GH * TPB
                nc.vector.memset(shift_cols[:, :], 0.0).then_inc(shift_rows_ready, 1)
                ve.wait_ge(shift_rows_ready, 1)
                with ve.Fori(0, NI) as i:
                    for u in range(2 * nq):
                        ve.wait_ge(max_scores, 2 * nq * i + (u + 1))
                        h = u % 2
                        nc.vector.tensor_reduce(half_max[:, u // 2, h:h + 1], PS[:, 2 * h:2 * h + 2, :], AX.XY,
                                                ALU.max, negate=True).then_inc(max_reduced, 1)
                    ve.wait_ge(max_reduced, 2 * nq * i + 2 * nq)
                    nc.vector.tensor_tensor(neg_max[:, :], half_max[:, :, 0], half_max[:, :, 1],
                                            ALU.min).then_inc(max_steps, 1)
                    ve.wait_ge(max_steps, 5 * i + 1)
                    nc.vector.tensor_copy(shift_parts[:, 0, :], neg_max[:, :]).then_inc(max_steps, 1)
                    ve.wait_ge(max_steps, 5 * i + 2)
                    nc.vector.tensor_tensor(neg_rest[:, :], neg_max[:, :], shift_parts[:, 0, :],
                                            ALU.subtract).then_inc(max_steps, 1)
                    ve.wait_ge(max_steps, 5 * i + 3)
                    nc.vector.tensor_copy(shift_parts[:, 1, :], neg_rest[:, :]).then_inc(max_steps, 1)
                    ve.wait_ge(max_steps, 5 * i + 4)
                    nc.vector.tensor_tensor(shift_parts[:, 2, :], neg_rest[:, :], shift_parts[:, 1, :],
                                            ALU.subtract).then_inc(max_steps, 1)
                    ve.wait_ge(shift_psum, i + 1)
                    nc.vector.tensor_copy(shift_rows[:, :], PS[:, MISC, 0:P // 2].bitcast(bf16)
                                          ).then_inc(shift_rows_ready, 1)
                    ve.wait_ge(shift_in, 16 * SPLIT * i + 16 * SPLIT)

            def drain_attention(i):
                ve.wait_ge(probs_used, NT * i + NT)
                nc.vector.transpose(oT[:, :, :].rearrange("p b d -> p (b d)"), PS[:, ACC, :]).then_inc(acc_free, 1)
                ve.wait_ge(acc_free, i + 2)
                nc.vector.reciprocal(rden[:, :, :], oT[:, :, HD:VW]).then_inc(attn_steps, 1)
                ve.wait_ge(attn_steps, 2 * i + 1)
                nc.vector.tensor_tensor(attn[:, i % NB, :, bass.ds((i // NB) * HD, HD)], oT[:, :, 0:HD],
                                        rden[:, :, :].to_broadcast([P, BLK // 32, HD]),
                                        ALU.mult).then_inc(attn_steps, 1)
                ve.wait_ge(attn_steps, 2 * i + 2)

            with ve.Fori(0, W_FREE) as i:
                drain_attention(i)
            ve.wait_ge(ffn_loaded, 16)
            QUARTER = FFN_COLS // QUARTERS
            for k in range(QUARTERS):
                cols = slice(QUARTER * k, QUARTER * (k + 1))
                steps.then_wait(nc.vector.tensor_copy(w_hi[:, cols], w_raw[:, cols]))
                nc.vector.tensor_tensor(w_lo[:, cols], w_raw[:, cols], w_hi[:, cols].bitcast(fp32),
                                        ALU.subtract).then_inc(w_split, 1)
            ve.wait_ge(w_split, QUARTERS)
            drain_attention(W_FREE)
            for k in range(QUARTERS):
                part = w_lo[:, QUARTER * k:QUARTER * (k + 1)].bitcast(fp32)
                nc.vector.tensor_reduce(low_range[:, 0, k:k + 1], part, AX.X, ALU.max)
                last = nc.vector.tensor_reduce(low_range[:, 1, k:k + 1], part, AX.X, ALU.min, negate=True)
            steps.then_wait(last)
            steps.then_wait(nc.vector.reduce_max(low_nonzero[:, :], low_range[:, :, :].rearrange("p s k -> p (s k)"),
                                                 AX.X))
            nc.vector.tensor_scalar(low_nonzero[:, :], low_nonzero[:, :], 0.0, None, ALU.is_gt).then_inc(low_any, 1)
            drain_attention(W_FREE + 1)
            ve.wait_ge(inexact_psum, 1)
            nc.vector.tensor_scalar(inexact[:, :], PS[0:1, MISC, 0:1], INEXACT, None, ALU.is_gt
                                    ).then_inc(inexact_ready, 1)

            def statistics(n, src):
                for t in range(TPB):
                    last = nc.vector.bn_stats(stats[:, 0, t, :], src[:, t, :])
                steps.then_wait(last)
                for t in range(TPB):
                    last = nc.vector.bn_aggr(mv[:, n % NB, t, :], stats[:, 0, t, :])
                last.then_inc(var_ready, 1)

            def apply_norm(n, dst, src):
                ve.wait_ge(rstd_ready, NB + n + 1)
                for t in range(TPB):
                    last = nc.vector.tensor_scalar(dst[:, t, :], src[:, t, :], mv[:, n % NB, t, 0:1],
                                                   rstd[:, n % NB, t:t + 1], ALU.subtract, ALU.mult)
                return last

            def centre(n, dst, src):
                ve.wait_ge(var_ready, NB + n + 1)
                for t in range(TPB):
                    last = nc.vector.tensor_scalar(dst[:, t, :], src[:, t, :], mv[:, n % NB, t, 0:1], None,
                                                   ALU.subtract)
                return last

            def scale_and_add(n, dst, centred, residue):
                for t in range(TPB):
                    last = nc.vector.scalar_tensor_tensor(dst[:, t, :], centred[:, t, :], rstd[:, n % NB, t:t + 1],
                                                          residue[:, t, :], ALU.mult, ALU.add)
                return last

            def untranspose(b):
                if b:
                    ve.wait_ge(proj_psum, b)
                nc.vector.transpose(oTn[:, :], attn[:, b, :, :].rearrange("p t d -> p (t d)")).then_inc(oTn_ready, 1)

            def attn_out(b):
                ve.wait_ge(proj_psum, b + 1)
                ve.wait_ge(rest_loaded, 16)
                for t in range(TPB):
                    last = nc.vector.tensor_tensor(ao[:, t, :], PS[:, MISC, D * t:D * (t + 1)],
                                                   rest[:, X_BO:X_BO + D], ALU.add)
                last.then_inc(proj_drained, 1)
                ve.wait_ge(proj_drained, b + 1)
                statistics(2 * b, ao)
                steps.then_wait(centre(2 * b, ln, ao))

            def residual(b):
                ve.wait_ge(rstd_ready, NB + 2 * b + 1)
                ve.wait_ge(x_again[b % 2], 16 * (b // 2 + 1))
                scale_and_add(2 * b, x1(b), ln, xr[:, b % 2, :, :]).then_inc(x1_ready, 1)
                ve.wait_ge(x1_ready, b + 1)
                statistics(2 * b + 1, x1(b))

            def second_norm(b):
                apply_norm(2 * b + 1, ln2, x1(b)).then_inc(ln2_ready, 1)

            def drain_xT(b):
                ve.wait_ge(xT_psum, b + 1)
                steps.then_wait(nc.vector.tensor_copy(xT_hi[:, tokens(b)], PS[:, MISC, :]))
                nc.vector.tensor_tensor(xT_lo[:, tokens(b)], PS[:, MISC, :], xT_hi[:, tokens(b)].bitcast(fp32),
                                        ALU.subtract).then_inc(xT_ready, 1)
                ve.wait_ge(xT_ready, b + 1)

            def gate(n):
                b, c = divmod(n, FC)
                ve.wait_ge(gate_psum, 2 * n + 2)
                ve.wait_ge(silu_ready, n + 1)
                nc.vector.scalar_tensor_tensor(h_raw[b][:, c, :], PS[:, 2 + n % 2, :],
                                               rest[:, X_S + FC + c:X_S + FC + c + 1], silu[:, n % SILUS, :],
                                               ALU.mult, ALU.mult).then_inc(gated_ready, 1)

            chain = (untranspose, attn_out, residual, second_norm, drain_xT)
            for b in range(NB - 1):
                for stage in chain:
                    stage(b)
                drain_attention(EARLY + b)
            after = {("G", 2, 1): untranspose, ("G", 2, 3): attn_out, ("B", 0, 0): residual,
                     ("B", 0, 1): second_norm, ("B", 1, 1): drain_xT}
            for kind, b, c in STEPS:
                if kind == "G":
                    gate(FC * b + c)
                elif kind in "BC":
                    hi, raw, lo = hidden_dst(kind, b)
                    ve.wait_ge(h_high, SPLITS.index((kind, b, c)) + 1)
                    nc.vector.tensor_tensor(lo[:, c, :], raw[:, c, :], hi[:, c, :].bitcast(fp32),
                                            ALU.subtract).then_inc(h_low, 1)
                if (kind, b, c) in after:
                    after[(kind, b, c)](NB - 1)
                if kind == "Z":
                    ve.wait_ge(y_tokens, b + 1)
                    y = PS[:, 2 + b % 2, :].rearrange("p (t d) -> p t d", d=D)
                    statistics(2 * NB + b, y)
                    centre(2 * NB + b, ln, y).then_inc(y_drained, 1)
                if kind == "A":
                    ve.wait_ge(y_drained, b + 1)
                    ve.wait_ge(rstd_ready, NB + 2 * NB + b + 1)
                    scale_and_add(2 * NB + b, x1(b), ln, x1(b)).then_inc(y_ready, 1)
                    ve.wait_ge(y_ready, b + 1)

        @block.tensor
        def _(pe):
            mm = nc.tensor.matmul

            def weight(col):
                return wp[:, col:col + D]

            def keep_warm(n, bank):
                for _ in range(n):
                    mm(PS[:, bank, :], warm[:, 0:P], warm[:, :], start=True, stop=True)

            def transpose_tiles(bank, src):
                for t in range(TPB):
                    last = nc.tensor.transpose(PS[:, bank, D * t:D * (t + 1)], src[:, t, :], ident[:, :])
                return last

            def transpose_x(b):
                pe.wait_ge(xn_ready, b + 1)
                if b:
                    pe.wait_ge(xnT_ready, b)
                transpose_tiles(MISC, xs[:, tiles(b), :]).then_inc(xnT_psum, 1)

            def down(b):
                pe.wait_ge(xnT_ready, b + 1)
                if b:
                    pe.wait_ge(ct_ready, b)
                mm(PS[:, ACC, :], weight(W_D), xnT[:, tokens(b)], start=True, stop=True).then_inc(ct_psum, 1)

            def project_side(m):
                kind, b = SIDES[m]
                content, rotated, swapped = side_banks(m)
                src, cols = (xnT, (W_KC, W_KR, W_KS)) if kind == K_SIDE else (ct, (W_QC, W_QR, W_QS))
                if m >= 2:
                    pe.wait_ge(side_drained, m - 1)
                if kind == Q_SIDE:
                    pe.wait_ge(ct_ready, b + 1)
                mm(PS[:, rotated, :], weight(cols[1]), src[:, tokens(b)], start=True, stop=True)
                mm(PS[:, swapped, :], weight(cols[2]), src[:, tokens(b)], start=True, stop=True)
                pe.wait_ge(ct_ready, b + 1)
                mm(PS[:, content, :], weight(cols[0]), ct[:, tokens(b)], start=True, stop=True).then_inc(side_psum, 1)

            def project_v(b):
                if b < 2:
                    pe.wait_ge(ct_ready, NB)
                elif b == 2:
                    pe.wait_ge(v_drained, 2)
                else:
                    pe.wait_ge(side_drained, NB + 3)
                for t in range(TPB):
                    at = b * BLK + t * P
                    last = mm(PS[:, v_bank(b), D * t:D * (t + 1)], ct[:, at:at + P], weight(W_V), start=True, stop=True)
                last.then_inc(v_psum, 1)

            def norm(m):
                pe.wait_ge(squares_ready, m + 1)
                for t in range(TPB):
                    kind, b = SIDES[m]
                    at, n = b * BLK + P * t, H * (NT * kind + TPB * b + t)
                    last = mm(PS[:, MISC, n:n + H], squares[:, kind, at:at + P], sel_bf, start=True, stop=True)
                last.then_inc(norm_psum, 1)

            pe.wait_ge(pool_constants, 1)
            keep_warm(WARM_START, 0)
            pe.wait_ge(ident_loaded, 16)
            transpose_x(0)
            pe.wait_ge(weights_loaded, 16)
            down(0)
            transpose_x(1)
            project_side(0)
            for b in range(1, NB):
                project_side(b)
                down(b)
                if b + 1 < NB:
                    transpose_x(b + 1)
            project_side(NB)
            project_v(0)
            project_v(1)
            project_side(NB + 1)
            project_side(NB + 2)
            pe.wait_ge(act_constants, 2)
            pe.wait_ge(v_drained, 1)
            for m in range(NB + 1):
                norm(m)
            project_side(NB + 3)
            project_v(2)
            norm(NB + 1)
            project_v(3)
            norm(NB + 2)
            keep_warm(WARM_NORM, 0)
            norm(NB + 3)

            pe.wait_ge(norm_reduced, 1)
            for s in range(2):
                last = mm(PS[0:1, 0, P * s:P * (s + 1)], norm_max[:, s:s + 1], ident[:, :], start=True, stop=True)
            last.then_inc(side_max_psum, 1)

            keep_warm(WARM_FLAG, 5)
            pe.wait_ge(flag_ready, 1)
            general = pe.value_load(unsafe[0:1, 0:1], min_val=0, max_val=1)
            with pe.If(general > 0):
                nq = GH * TPB
                pe.wait_ge(operands_in, operands_of(NI - 1))
                with pe.Fori(0, NI) as i:
                    for u in range(2 * nq):
                        j, t, h = u // (2 * TPB), u // 2 % TPB, u % 2
                        if u >= 2:
                            pe.wait_ge(max_reduced, 2 * nq * i + (u - 1))
                        for k in range(2):
                            last = mm(PS[:, 2 * h + k, :], QT[:, i, j, P * t:P * (t + 1)],
                                      KT[:, i // NB, j, (2 * h + k) * BLK:(2 * h + k + 1) * BLK],
                                      start=True, stop=True)
                        last.then_inc(max_scores, 1)
                    pe.wait_ge(max_steps, 5 * i + 5)
                    pe.wait_ge(shift_rows_ready, i + 1)
                    nc.tensor.transpose(PS[:, MISC, 0:P // 2].bitcast(bf16), shift_cols[:, :],
                                        ident_bf[:, :]).then_inc(shift_psum, 1)
                pe.wait_ge(shift_in, 16 * SPLIT * NI)

            def fill(i, t, half):
                dst = unit((2 * NT * i + (2 * t + half)) % UNITS)
                for k in range(2):
                    j = 2 * half + k
                    last = mm(dst[:, BLK * k:BLK * (k + 1)], KT[:, i // NB, j, P * t:P * (t + 1)], QT[:, i, j, :],
                              start=True, stop=True)
                last.then_inc(scores_ready, 1)

            def attend(i, inserts):
                filling_next = not (isinstance(i, int) and i == NI - 1)
                for t in range(NT):
                    ahead = t + 2
                    fi, ft = (i, ahead) if ahead < NT else (i + 1, ahead - NT)
                    filling = ahead < NT or filling_next
                    if filling:
                        if ahead == NT:
                            pe.wait_ge(operands_in, operands_of(fi))
                        pe.wait_ge(probs_ready, 2 * NT * i + (2 * ahead - 2))
                        fill(fi, ft, 0)
                    pe.wait_ge(probs_ready, 2 * NT * i + (2 * t + 2))
                    if t == 0:
                        pe.wait_ge(acc_free, i + 1)
                        pe.wait_ge(v_staged, 2 * (i // NB) + 1)
                    if t == NT // 2:
                        pe.wait_ge(v_staged, 2 * (i // NB) + 2)
                    for j in range(GH):
                        last = mm(PS[32 * j:32 * j + VW, ACC, :], Vst[:, t, VW * j:VW * (j + 1)], probs[:, t % SLOTS, j, :],
                                  start=t == 0, stop=t == NT - 1)
                    last.then_inc(probs_used, 1)
                    if filling:
                        pe.wait_ge(probs_ready, 2 * NT * i + (2 * ahead - 1))
                        fill(fi, ft, 1)
                    if t in inserts:
                        inserts[t]()

            def project(b):
                pe.wait_ge(oTn_ready, b + 1)
                pe.wait_ge(rest_loaded, 16)
                if b:
                    pe.wait_ge(xT_ready, b)
                else:
                    pe.wait_ge(inexact_ready, 1)
                for t in range(TPB):
                    last = mm(PS[:, MISC, D * t:D * (t + 1)], oTn[:, P * t:P * (t + 1)], rest[:, X_WO:X_WO + D],
                              start=True, stop=True)
                last.then_inc(proj_psum, 1)

            def count_inexact():
                pe.wait_ge(low_any, 1)
                mm(PS[0:1, MISC, 0:1], low_nonzero[:, :], ones[:, :], start=True, stop=True).then_inc(inexact_psum, 1)

            def transpose_x2(b):
                pe.wait_ge(ln2_ready, b + 1)
                transpose_tiles(MISC, ln2).then_inc(xT_psum, 1)

            pe.wait_ge(acc_free, 1)
            pe.wait_ge(operands_in, operands_of(0))
            fill(0, 0, 0)
            fill(0, 0, 1)
            fill(0, 1, 0)
            pe.wait_ge(probs_ready, 1)
            fill(0, 1, 1)
            with pe.Fori(0, EARLY) as i:
                attend(i, {})
            attend(EARLY, {2: count_inexact, 6: lambda: project(0), 13: lambda: transpose_x2(0)})
            some_low = pe.value_load(inexact[0:1, 0:1], min_val=0, max_val=1)
            attend(EARLY + 1, {6: lambda: project(1), 13: lambda: transpose_x2(1)})
            attend(EARLY + 2, {6: lambda: project(2), 13: lambda: transpose_x2(2)})

            def feed_forward(with_low):
                def product(out_ap, at, rhs_hi, rhs_lo, start, stop):
                    hi, lo = w_hi[:, at:at + P], w_lo[:, at:at + P]
                    mm(out_ap, hi, rhs_hi, start=start, stop=False)
                    last = mm(out_ap, hi, rhs_lo, start=False, stop=stop and not with_low)
                    if with_low:
                        last = mm(out_ap, lo, rhs_hi, start=False, stop=stop)
                    return last

                def gates(n):
                    b, c, slot = n // FC, n % FC, n % 2
                    if c == 0:
                        pe.wait_ge(xT_ready, b + 1)
                    if n >= 2:
                        pe.wait_ge(silu_ready, n - 1)
                    product(PS[:, slot, :], X_W1 + P * c, xT_hi[:, tokens(b)], xT_lo[:, tokens(b)],
                            True, True).then_inc(gate_psum, 1)
                    if n >= 2:
                        pe.wait_ge(gated_ready, n - 1)
                    product(PS[:, 2 + slot, :], X_W2 + P * c, xT_hi[:, tokens(b)], xT_lo[:, tokens(b)],
                            True, True).then_inc(gate_psum, 1)

                pe.wait_ge(w_split, QUARTERS)
                for kind, b, c in PE_STEPS:
                    if kind == "G":
                        gates(FC * b + c)
                        if (b, c) == (2, 3):
                            project(NB - 1)
                    elif kind in "BC":
                        n = HIDDEN.index((kind, b, c))
                        hi, lo = hidden_src(kind, b)
                        w = X_H1 if kind == "B" else X_H2
                        if n >= 3:
                            pe.wait_ge(gelu_ready, n - 2)
                        elif n == 2:
                            pe.wait_ge(acc_free, NI + 1)
                        for k in range(FC):
                            if c == 0:
                                pe.wait_ge(*split_done(kind, b, k))
                            last = product(PS[:, hidden_bank(n), :], w + F * k + P * c, hi[:, k, :], lo[:, k, :],
                                           k == 0, k == FC - 1)
                        last.then_inc(hidden_psum, 1)
                        if (kind, b, c) == ("B", 1, 1):
                            transpose_x2(NB - 1)
                    elif kind == "Y":
                        hi, lo = hidden_src(kind, b)
                        if b >= 2:
                            pe.wait_ge(yT_ready, b - 1)
                        for k in range(FC):
                            pe.wait_ge(*split_done(kind, b, k))
                            last = product(PS[:, b % 2, :], X_W3 + D * k, hi[:, k, :], lo[:, k, :],
                                           k == 0, k == FC - 1)
                        last.then_inc(y_psum, 1)
                    elif kind == "Z":
                        pe.wait_ge(yT_ready, b + 1)
                        if b >= 2:
                            pe.wait_ge(y_drained, b - 1)
                        transpose_tiles(2 + b % 2, yT[:, b % 2, :].rearrange("p (t n) -> p t n", n=P)
                                        ).then_inc(y_tokens, 1)

            with pe.If(some_low > 0):
                feed_forward(True)
            with pe.If(some_low < 1):
                feed_forward(False)


FEATURES = np.arange(D).reshape(NG, GH, HD).transpose(0, 2, 1).reshape(D)


def setup_pack(i):
    a = {k[len("L0_attn_"):]: np.asarray(v) for k, v in i.items() if k.startswith("L0_attn_")}
    R = D // 2
    pack = np.zeros((P, SETUP_COLS), np.float32)

    def swapped(w):
        return w.reshape(w.shape[:-1] + (D // 2, 2))[..., ::-1].reshape(w.shape)[..., FEATURES]

    pack[:, W_D:W_D + R], pack[:, W_D + R:W_D + D] = a["Wd_q_w"], a["Wd_kv_w"]
    pack[:R, W_QC:W_QC + D] = a["Wu_q_w"][:, FEATURES]
    pack[:R, W_QR:W_QR + D] = a["Wq_r_w"][:, FEATURES]
    pack[:R, W_QS:W_QS + D] = swapped(a["Wq_r_w"])
    pack[R:, W_KC:W_KC + D] = a["Wu_k_w"][:, FEATURES]
    pack[:, W_KR:W_KR + D] = a["Wk_r_w"][:, FEATURES]
    pack[:, W_KS:W_KS + D] = swapped(a["Wk_r_w"])
    pack[R:, W_V:W_V + D] = a["Wu_v_w"]
    pack[:, B_V:B_V + D] = a["Wu_v_b"]
    pack[np.arange(D), SEL + FEATURES // HD] = 1
    pack[:R, BIAS], pack[R:, BIAS] = a["Wd_q_b"], a["Wd_kv_b"]
    for n, b in enumerate((a["Wu_q_b"][FEATURES], a["Wq_r_b"][FEATURES], swapped(a["Wq_r_b"]),
                           a["Wu_k_b"][FEATURES], a["Wk_r_b"][FEATURES], swapped(a["Wk_r_b"]))):
        pack[:, BIAS + 1 + n] = b
    return pack


def ffn_pack(i):
    f = {k[len("L0_ffn_"):]: np.asarray(v) for k, v in i.items() if k.startswith("L0_ffn_")}
    pack = np.zeros((P, FFN_COLS), np.float32)
    pack[:, X_W1:X_W1 + F], pack[:, X_W2:X_W2 + F] = f["w1_w"].T, f["w2_w"].T
    for k in range(FC):
        pack[:, X_H1 + F * k:X_H1 + F * (k + 1)] = f["h1_w"].T[P * k:P * (k + 1)]
        pack[:, X_H2 + F * k:X_H2 + F * (k + 1)] = f["h2_w"].T[P * k:P * (k + 1)]
        pack[:, X_W3 + D * k:X_W3 + D * (k + 1)] = f["w3_w"].T[P * k:P * (k + 1)]
    return pack


def rest_pack(i):
    pack = np.zeros((P, REST_COLS), np.float32)
    wo = np.asarray(i["L0_attn_Wo_w"])
    for g in range(NG):
        for j in range(GH):
            r = HD * (GH * g + j)
            at = 32 * j + HD * g
            pack[at:at + HD, X_WO:X_WO + D] = wo[r:r + HD]
    pack[:, X_BO:X_BO + D] = np.asarray(i["L0_attn_Wo_b"])
    for n, name in enumerate(("w1_s", "w2_s", "h1_s", "h2_s")):
        pack[:, X_S + FC * n:X_S + FC * (n + 1)] = np.asarray(i["L0_ffn_" + name]).reshape(FC, P).T
    pack[:, X_S + 4 * FC] = np.asarray(i["L0_ffn_w3_s"])
    return pack


def rotation_tables():
    pos = np.arange(T, dtype=np.float32)
    ids = np.arange(D // 2, dtype=np.float32)
    theta = (np.float32(10000.0) ** (np.float32(-2.0) * ids)).astype(np.float32) / np.float32(D // 2)
    angle = theta[:, None] * pos[None, :]
    cos = np.repeat(np.cos(angle), 2, axis=0).astype(np.float32)
    sin = np.repeat(np.sin(angle), 2, axis=0).astype(np.float32)
    sin[0::2] = -sin[0::2]
    return np.ascontiguousarray(cos[FEATURES]), np.ascontiguousarray(sin[FEATURES])


def kernel(**inputs):
    import concourse.bacc as bacc
    from concourse.bass_utils import run_bass_kernel_spmd

    cos, sin = rotation_tables()
    arrays = {
        "x": np.ascontiguousarray(np.asarray(inputs["L0_attn_x"])[0]),
        "setup": setup_pack(inputs),
        "ffn": ffn_pack(inputs),
        "rest_of_tail": rest_pack(inputs),
        "cos": cos,
        "sin": sin,
        "identity": np.eye(P, dtype=np.float32),
    }
    nc = bacc.Bacc("TRN2", target_bir_lowering=False, num_devices=1)
    fp32 = mybir.dt.float32
    args = [nc.dram_tensor(name, a.shape, fp32, kind="ExternalInput").ap() for name, a in arrays.items()]
    for name, shape in (("q_scratch", (NB, SPLIT, SPLIT, D, BLK)), ("k_scratch", (SPLIT, D, T))):
        args.append(nc.dram_tensor(name, shape, mybir.dt.bfloat16, kind="Internal").ap())
    args.append(nc.dram_tensor("out", (T, D), fp32, kind="ExternalOutput").ap())
    layer(nc, *args)
    result = run_bass_kernel_spmd(nc, [arrays], core_ids=[0])
    return result.results[0]["out"].reshape(1, T, D)
```
